# Optimizing a Trainium2 kernel written in Bass

```python
import numpy as np
import jax
import jax.numpy as jnp

def _softmax(x, axis=-1):
    return jax.nn.softmax(x, axis=axis)

def _gelu(x):
    return jax.nn.gelu(x, approximate=True)

def _silu(x):
    return jax.nn.silu(x)

def _sigmoid(x):
    return jax.nn.sigmoid(x)

def _layernorm(x, axis=-1, eps=1e-05):
    m = jnp.mean(x, axis=axis, keepdims=True)
    v = jnp.var(x, axis=axis, keepdims=True)
    return (x - m) / jnp.sqrt(v + eps)

def _scatter_add(tgt, idx, src, axis=0):
    return tgt.at[idx].add(src)

def _segment_sum(src, seg, n):
    return jax.ops.segment_sum(src, seg, n)
kernel_name = 'mk_gps_d1_gnn_r8_88f187'

def setup_inputs(seed: int=0):
    np.random.seed(seed)
    _w = jnp.asarray

    def _rec_inputs():
        import jax
        import jax.numpy as jnp
        _gk = jax.random.key(seed)
        x = -0.0006008 + 1.001 * jax.random.normal(jax.random.fold_in(_gk, 1), (12500, 256), jnp.float32)
        _s = jax.random.randint(jax.random.fold_in(_gk, 2), (100000,), 0, 12500, jnp.int32)
        _d = jax.random.randint(jax.random.fold_in(_gk, 3), (100000,), 0, 12500, jnp.int32)
        _loop = jnp.arange(12500, dtype=jnp.int32)
        src = jnp.concatenate([_s, _d, _loop])
        dst = jnp.concatenate([_d, _s, _loop])
        _o = jnp.argsort(dst, stable=True)
        src = src[_o]
        dst = dst[_o]
        return (x, src, dst)
    x, src, dst = _rec_inputs()

    def _L0_gnn_setup():
        import jax, jax.numpy as jnp
        import numpy as np
        N_NODES = 1250
        N_EDGES = 40000
        D_IN = 256
        D_OUT = 256
        key = jax.random.key(seed)
        k1, k2, k3, k4 = jax.random.split(key, 4)
        x = jax.random.normal(k1, (N_NODES, D_IN), dtype=jnp.float32)
        edge_index = jax.random.randint(k2, (2, N_EDGES), 0, N_NODES, dtype=jnp.int64)
        weight = jax.random.normal(k3, (2 * D_IN, D_OUT), dtype=jnp.float32) / np.sqrt(2 * D_IN)
        bias = jax.random.normal(k4, (D_OUT,), dtype=jnp.float32)
        return {'x': x, 'edge_index': edge_index, 'weight': weight, 'bias': bias}
    _L0_gnn_all = _L0_gnn_setup()
    _L0_gnn_in = {k: v for k, v in _L0_gnn_all.items() if k in ('weight', 'bias')}
    del _L0_gnn_all

    def _L0_mix_setup():
        import jax, jax.numpy as jnp
        import numpy as np
        HEADS = 8
        DIM_HEAD = 64
        EPS = 1e-05

        def _inst_norm_lastdim(t):
            mu = jnp.mean(t, axis=-1, keepdims=True)
            var = jnp.mean(jnp.square(t - mu), axis=-1, keepdims=True)
            return (t - mu) * jax.lax.rsqrt(var + EPS)
        key = jax.random.key(seed)
        k1, k2, k3, k4 = jax.random.split(key, 4)
        b, n, dim = (4, 1024, 256)
        inner = HEADS * DIM_HEAD
        x = jax.random.normal(k1, (b, n, dim), dtype=jnp.float32)
        Wqkv = jax.random.normal(k2, (3 * inner, dim), dtype=jnp.float32) * (1.0 / np.sqrt(dim))
        Wout = jax.random.normal(k3, (dim, inner), dtype=jnp.float32) * (1.0 / np.sqrt(inner))
        bout = jax.random.normal(k4, (dim,), dtype=jnp.float32) * 0.01
        return {'x': x, 'Wqkv': Wqkv, 'Wout': Wout, 'bout': bout}
    _L0_mix_all = _L0_mix_setup()
    _L0_mix_in = {k: v for k, v in _L0_mix_all.items() if k in ('Wqkv', 'Wout', 'bout')}
    del _L0_mix_all

    def _L0_ffn_setup():
        import jax, jax.numpy as jnp
        import numpy as np
        B, N, D = (16, 512, 256)
        NUM_EXPERTS, TOP_K, HEADS = (4, 2, 4)
        N_EDGES = 131072
        LN_EPS = 1e-05

        def _layernorm(x, g, b):
            mu = x.mean(-1, keepdims=True)
            var = ((x - mu) ** 2).mean(-1, keepdims=True)
            return (x - mu) * jax.lax.rsqrt(var + LN_EPS) * g + b

        def _forward(x, edge_index, W_gat, att_src, att_dst, b_gat, ln_gamma, ln_beta, W1, b1, W2, b2):
            Bc, Nc, Dc = x.shape
            M = Bc * Nc
            x_flat = x.reshape(M, Dc)
            h = (x_flat @ W_gat).reshape(M, HEADS, NUM_EXPERTS)
            loops = jnp.arange(M, dtype=edge_index.dtype)
            src = jnp.concatenate([edge_index[0], loops])
            dst = jnp.concatenate([edge_index[1], loops])
            a_src = (h * att_src).sum(-1)
            a_dst = (h * att_dst).sum(-1)
            e = jax.nn.leaky_relu(a_src[src] + a_dst[dst], negative_slope=0.2)
            e_max = jax.ops.segment_max(e, dst, num_segments=M)
            ee = jnp.exp(e - e_max[dst])
            denom = jax.ops.segment_sum(ee, dst, num_segments=M)
            alpha = ee / (denom[dst] + 1e-16)
            msg = h[src] * alpha[:, :, None]
            agg = jax.ops.segment_sum(msg, dst, num_segments=M).reshape(M, HEADS * NUM_EXPERTS) + b_gat
            scores = _layernorm(agg, ln_gamma, ln_beta).reshape(M, HEADS, NUM_EXPERTS).mean(1)
            scores = scores.reshape(Bc, Nc, NUM_EXPERTS)
            topk_s, topk_i = jax.lax.top_k(scores, TOP_K)
            w = jax.nn.softmax(topk_s, axis=-1)
            out = jnp.zeros_like(x)
            for ei in range(NUM_EXPERTS):
                g = jnp.where(topk_i == ei, w, 0.0).sum(-1)
                hh = jax.nn.gelu(x @ W1[ei] + b1[ei], approximate=False)
                out = out + g[..., None] * (hh @ W2[ei] + b2[ei])
            return out
        key = jax.random.key(seed)
        ks = jax.random.split(key, 8)
        s = 0.05
        return {'x': jax.random.normal(ks[0], (B, N, D), jnp.float32), 'W_gat': jax.random.normal(ks[1], (D, HEADS * NUM_EXPERTS), jnp.float32) * s, 'att_src': jax.random.normal(ks[2], (HEADS, NUM_EXPERTS), jnp.float32) * s, 'att_dst': jax.random.normal(ks[3], (HEADS, NUM_EXPERTS), jnp.float32) * s, 'b_gat': jnp.zeros((HEADS * NUM_EXPERTS,), jnp.float32), 'ln_gamma': jnp.ones((HEADS * NUM_EXPERTS,), jnp.float32), 'ln_beta': jnp.zeros((HEADS * NUM_EXPERTS,), jnp.float32), 'W1': jax.random.normal(ks[4], (NUM_EXPERTS, D, 2 * D), jnp.float32) * s, 'b1': jnp.zeros((NUM_EXPERTS, 2 * D), jnp.float32), 'W2': jax.random.normal(ks[5], (NUM_EXPERTS, 2 * D, D), jnp.float32) * s, 'b2': jnp.zeros((NUM_EXPERTS, D), jnp.float32), 'edge_index': jax.random.randint(ks[6], (2, N_EDGES), 0, B * N, jnp.int32)}
    _L0_ffn_all = _L0_ffn_setup()
    _L0_ffn_in = {k: v for k, v in _L0_ffn_all.items() if k in ('W_gat', 'att_src', 'att_dst', 'b_gat', 'ln_gamma', 'ln_beta', 'W1', 'b1', 'W2', 'b2', 'edge_index')}
    del _L0_ffn_all
    return {'x': x, 'src': src, 'dst': dst, 'L0_gnn_weight': _L0_gnn_in['weight'], 'L0_gnn_bias': _L0_gnn_in['bias'], 'L0_mix_Wqkv': _L0_mix_in['Wqkv'], 'L0_mix_Wout': _L0_mix_in['Wout'], 'L0_mix_bout': _L0_mix_in['bout'], 'L0_ffn_W_gat': _L0_ffn_in['W_gat'], 'L0_ffn_att_src': _L0_ffn_in['att_src'], 'L0_ffn_att_dst': _L0_ffn_in['att_dst'], 'L0_ffn_b_gat': _L0_ffn_in['b_gat'], 'L0_ffn_ln_gamma': _L0_ffn_in['ln_gamma'], 'L0_ffn_ln_beta': _L0_ffn_in['ln_beta'], 'L0_ffn_W1': _L0_ffn_in['W1'], 'L0_ffn_b1': _L0_ffn_in['b1'], 'L0_ffn_W2': _L0_ffn_in['W2'], 'L0_ffn_b2': _L0_ffn_in['b2'], 'L0_ffn_edge_index': _L0_ffn_in['edge_index']}

def reference(x, src, dst, L0_gnn_weight, L0_gnn_bias, L0_mix_Wqkv, L0_mix_Wout, L0_mix_bout, L0_ffn_W_gat, L0_ffn_att_src, L0_ffn_att_dst, L0_ffn_b_gat, L0_ffn_ln_gamma, L0_ffn_ln_beta, L0_ffn_W1, L0_ffn_b1, L0_ffn_W2, L0_ffn_b2, L0_ffn_edge_index):
    import jax
    import jax.numpy as jnp

    def _L0_gnn_ref(x, edge_index, weight, bias):
        import jax, jax.numpy as jnp
        import numpy as np
        N_NODES = 1250
        N_EDGES = 40000
        D_IN = 256
        D_OUT = 256
        n = x.shape[0]
        src, dst = (edge_index[0], edge_index[1])
        summed = jax.ops.segment_sum(x[src], dst, num_segments=n)
        deg = jax.ops.segment_sum(jnp.ones_like(src, dtype=x.dtype), dst, num_segments=n)
        agg = summed / jnp.maximum(deg, 1.0)[:, None]
        out = jnp.concatenate([x, agg], axis=-1) @ weight
        out = out / jnp.linalg.norm(out, axis=-1, keepdims=True)
        return out + bias

    def _L0_mix_ref(x, Wqkv, Wout, bout):
        import jax, jax.numpy as jnp
        import numpy as np
        HEADS = 8
        DIM_HEAD = 64
        EPS = 1e-05

        def _inst_norm_lastdim(t):
            mu = jnp.mean(t, axis=-1, keepdims=True)
            var = jnp.mean(jnp.square(t - mu), axis=-1, keepdims=True)
            return (t - mu) * jax.lax.rsqrt(var + EPS)
        b, n, dim = x.shape
        qkv = jnp.einsum('bnc,fc->bnf', x, Wqkv)
        q, k, v = jnp.split(qkv, 3, axis=-1)

        def to_heads(t):
            return t.reshape(b, n, HEADS, DIM_HEAD).transpose(0, 2, 1, 3)
        q, k, v = (to_heads(q), to_heads(k), to_heads(v))
        k = _inst_norm_lastdim(k)
        v = _inst_norm_lastdim(v)
        dots = jnp.einsum('bhnd,bhne->bhde', k, v)
        out = jnp.einsum('bhnd,bhde->bhne', q, dots) / n
        out = out.transpose(0, 2, 1, 3).reshape(b, n, HEADS * DIM_HEAD)
        return jnp.einsum('bnf,cf->bnc', out, Wout) + bout

    def _L0_ffn_ref(x, W_gat, att_src, att_dst, b_gat, ln_gamma, ln_beta, W1, b1, W2, b2, edge_index):
        import jax, jax.numpy as jnp
        import numpy as np
        B, N, D = (16, 512, 256)
        NUM_EXPERTS, TOP_K, HEADS = (4, 2, 4)
        N_EDGES = 131072
        LN_EPS = 1e-05

        def _layernorm(x, g, b):
            mu = x.mean(-1, keepdims=True)
            var = ((x - mu) ** 2).mean(-1, keepdims=True)
            return (x - mu) * jax.lax.rsqrt(var + LN_EPS) * g + b

        def _forward(x, edge_index, W_gat, att_src, att_dst, b_gat, ln_gamma, ln_beta, W1, b1, W2, b2):
            Bc, Nc, Dc = x.shape
            M = Bc * Nc
            x_flat = x.reshape(M, Dc)
            h = (x_flat @ W_gat).reshape(M, HEADS, NUM_EXPERTS)
            loops = jnp.arange(M, dtype=edge_index.dtype)
            src = jnp.concatenate([edge_index[0], loops])
            dst = jnp.concatenate([edge_index[1], loops])
            a_src = (h * att_src).sum(-1)
            a_dst = (h * att_dst).sum(-1)
            e = jax.nn.leaky_relu(a_src[src] + a_dst[dst], negative_slope=0.2)
            e_max = jax.ops.segment_max(e, dst, num_segments=M)
            ee = jnp.exp(e - e_max[dst])
            denom = jax.ops.segment_sum(ee, dst, num_segments=M)
            alpha = ee / (denom[dst] + 1e-16)
            msg = h[src] * alpha[:, :, None]
            agg = jax.ops.segment_sum(msg, dst, num_segments=M).reshape(M, HEADS * NUM_EXPERTS) + b_gat
            scores = _layernorm(agg, ln_gamma, ln_beta).reshape(M, HEADS, NUM_EXPERTS).mean(1)
            scores = scores.reshape(Bc, Nc, NUM_EXPERTS)
            topk_s, topk_i = jax.lax.top_k(scores, TOP_K)
            w = jax.nn.softmax(topk_s, axis=-1)
            out = jnp.zeros_like(x)
            for ei in range(NUM_EXPERTS):
                g = jnp.where(topk_i == ei, w, 0.0).sum(-1)
                hh = jax.nn.gelu(x @ W1[ei] + b1[ei], approximate=False)
                out = out + g[..., None] * (hh @ W2[ei] + b2[ei])
            return out
        return _forward(x, edge_index, W_gat, att_src, att_dst, b_gat, ln_gamma, ln_beta, W1, b1, W2, b2)
    edge_index = jnp.stack([src, dst])
    xn = _layernorm(x, axis=-1)
    x = x + _L0_gnn_ref(xn, edge_index, L0_gnn_weight, L0_gnn_bias) + _L0_mix_ref(xn[None], L0_mix_Wqkv, L0_mix_Wout, L0_mix_bout)[0]
    x = x + _L0_ffn_ref(_layernorm(x, axis=-1)[None], L0_ffn_W_gat, L0_ffn_att_src, L0_ffn_att_dst, L0_ffn_b_gat, L0_ffn_ln_gamma, L0_ffn_ln_beta, L0_ffn_W1, L0_ffn_b1, L0_ffn_W2, L0_ffn_b2, L0_ffn_edge_index)[0]
    return x

_drawn_inputs = setup_inputs


def setup_inputs(seed=0):
    import zlib

    import numpy as np

    out = dict(_drawn_inputs(seed))
    spreads = {'L0_ffn_b_gat': (0.0, 0.1),
     'L0_ffn_ln_gamma': (1.0, 0.2),
     'L0_ffn_ln_beta': (0.0, 0.1),
     'L0_ffn_b1': (0.0, 0.1),
     'L0_ffn_b2': (0.0, 0.1)}
    factors = {'L0_mix_bout': 2.777, 'L0_ffn_att_src': 2.732, 'L0_ffn_att_dst': 5.257}
    for name, (base, spread) in spreads.items():
        noise = np.random.default_rng([zlib.crc32(name.encode()), seed]).standard_normal(out[name].shape)
        drawn = base * np.exp(spread * noise) if base else spread * noise
        out[name] = jnp.asarray(drawn.astype(out[name].dtype))
    for name, factor in factors.items():
        out[name] = (out[name] * factor).astype(out[name].dtype)
    return out
```

```python
import concourse.bass as bass
from concourse import mybir
from contextlib import ExitStack

f32 = mybir.dt.float32
i32 = mybir.dt.int32
bf16 = mybir.dt.bfloat16
ALU = mybir.AluOpType
ACT = mybir.ActivationFunctionType
AX = mybir.AxisListType

N, D = 12500, 256
NP = 125
NT = N // NP
P = 128
EG = 212500
EF = 131072
GC = 1664
GJ = GC // P
FC = EF // P
FJ = FC // P
HEADS, DH = 8, 64
INNER = HEADS * DH
NE, FH = 4, 512
RH = 4
ROW = 24
FAR = 16000.0
NEG = -1.0e30
MAGIC = 12582912.0
EPS = 1e-5
GU = 9
FU = 6
GW = GC + GU
LIST_BLOCKS = (EF // FU + NT + P) // P * P
BLK = NP * FU


def steps(eng, n, unroll, stages):
    depth = max(lag for lag, _ in stages)
    head = -(-depth // unroll) * unroll
    body = (n - head) // unroll

    def step(s, slot, static):
        for lag, emit in stages:
            if static is None or 0 <= static - lag < n:
                emit(s - lag, (slot - lag) % unroll)

    for s in range(head):
        step(s, s % unroll, s)
    with eng.Fori(0, body) as i:
        for u in range(unroll):
            step(i * unroll + (head + u), u, None)
    for s in range(head + body * unroll, n + depth):
        step(s, s % unroll, s)


def wait_after(eng, sem, value):
    if not (isinstance(value, int) and value <= 0):
        eng.wait_ge(sem, value)


def repeat(eng, count, body):
    with eng.If(count > 0):
        with eng.Fori(0, count) as i:
            body(i)


def to_all(row):
    return row.broadcast_to([P, row.shape[1]])


def along(a, n):
    return a.rearrange("p (m o) -> p m o", o=1).broadcast_to([a.shape[0], a.shape[1], n])


def row_of(a, n):
    return a.rearrange("(o f) -> o f", o=1).broadcast_to([NP, n])


def build(nc, x, src, dst, gnn_w, gnn_b, wqkv, wkv_t, wout_t, bout, w_gat, att_src, att_dst,
          b_gat, ln_g, ln_b, w1, b1, w2, b2, fedge, out, dbg=None):
    ctx = ExitStack()
    with ctx:
        sb = lambda name, shape, dt=f32: ctx.enter_context(nc.sbuf_tensor(name, shape, dt))
        pb = lambda name, shape, dt=f32: ctx.enter_context(nc.psum_tensor(name, shape, dt))
        sem = lambda name: ctx.enter_context(nc.semaphore(name))
        dram = lambda name, shape, dt=f32: nc.dram_tensor(name, shape, dt, kind="Internal").ap()

        xn_rows = dram("xn_rows", [N, D])
        x1_rows = dram("x1_rows", [N, D])
        route_rows = dram("route_rows", [N + 1, ROW])
        lists = dram("lists", [LIST_BLOCKS * BLK, 1], i32)
        xn_turned = dram("xn_turned", [NT, P, 2 * NP])
        x2_turned = dram("x2_turned", [NT, P, 2 * NP])
        hi_rows = dram("hi_rows", [FC, P], bf16)
        chunk_lo = dram("chunk_lo", [GC, 1])
        chunk_hi = dram("chunk_hi", [GC, 1])

        ident = sb("ident", [P, P])
        below = sb("below", [P, P])
        above = sb("above", [P, P])
        iota_j = sb("iota_j", [P, P])
        iota_p = sb("iota_p", [P, 1])
        neg_first = sb("neg_first", [P, NT])
        zeros_b = sb("zeros_b", [P, 512], bf16)
        eps_c = sb("eps_c", [P, 1])

        arena = sb("arena", [P, 8192])
        hi_e, lo_e, src_e, dst_e = (arena[:, k * FC:(k + 1) * FC] for k in range(4))
        wkv = arena[:, 4096:6144].rearrange("p (k f) -> p k f", k=2)
        wq = arena[:, 6144:7168].rearrange("p (k f) -> p k f", k=4)
        wo = arena[:, 7168:8192].rearrange("p (k f) -> p k f", k=4)
        w1_sb = arena[:, 0:4096].rearrange("p (k e f) -> p k e f", k=2, e=NE)
        w2_sb = arena[:, 4096:8192].rearrange("p (e k f) -> p e k f", e=NE, k=4)
        wg = sb("wg", [P, 4, D])
        mix = sb("mix", [P, 2, D])
        wr = sb("wr", [P, 2, ROW])
        att = sb("att", [P, 2, 16])
        bias_x = sb("bias_x", [P, D])
        bout_b = sb("bout_b", [P, D])
        gsrc = sb("gsrc", [P, GW], i32)
        gdst = sb("gdst", [P, GW])
        adst = sb("adst", [NP, NT, RH])
        gplan = sb("gplan", [1, 3 * NT], i32)
        fplan = sb("fplan", [1, 2 * NT + 1], i32)

        s_const = sem("s_const")
        s_w = sem("s_w")
        s_v = sem("s_v")
        s_gate = sem("s_gate")
        PS = [pb(f"PS{k}", [P, 512]) for k in range(8)]

        small = sb("small", [P, 64])
        pad_list = sb("pad_list", [P, BLK], i32)
        base8 = sb("base8", [P, 1])

        oh_hi = sb("oh_hi", [P, 8, NT], bf16)
        oh_lo = sb("oh_lo", [P, 8, NP], bf16)
        dst_b = [sb(f"dst_b{h}", [P, 512], i32) for h in range(2)]
        hi_bc = [sb(f"hi_bc{h}", [P, 512], bf16) for h in range(2)]
        oh_t = [sb(f"oh_t{h}", [NT, 512]) for h in range(2)]
        t_sb = sb("t_sb", [NT, NP])
        rk = sb("rk", [P, 8])
        tv = sb("tv", [P, 8])
        junk = sb("junk", [P, 8, P], bf16)
        junk_l = sb("junk_l", [P, 8, P], bf16)
        pos_f = sb("pos_f", [P, 8])
        blk_f = sb("blk_f", [P, 8])
        pos_i = sb("pos_i", [P, 8], i32)
        val_i = sb("val_i", [P, 8], i32)

        setup = ExitStack()
        flat = setup.enter_context(nc.sbuf_tensor("flat", [P, 2 * N], f32))[:]
        at = [0]

        def take(cols, dt=f32):
            v = flat[:, at[0]:at[0] + cols]
            at[0] += cols
            assert at[0] <= 2 * N
            return v if dt == f32 else v.bitcast(dt)

        tiles = lambda v: v.rearrange("p (j e) -> p j e", e=P)
        gd_i, gs_i = tiles(take(GC, i32)), tiles(take(GC, i32))
        g_f, gs_f = tiles(take(GC)), tiles(take(GC))
        fd_i, fs_i = tiles(take(FC, i32)), tiles(take(FC, i32))
        f_d, f_s, f_hi, f_lo = (tiles(take(FC)) for _ in range(4))
        f_hib = tiles(take(FC // 2, bf16))
        gh, gt = tiles(take(GC)), tiles(take(GC))
        lo_b, hi_b = flat[:, 0:GC], flat[:, GC:2 * GC]
        m_b, chunk_no, cand = take(GC), take(GC), take(GC)

        CNT, SM = PS[2], PS[3]

        turned = []
        for of, to, n in ((f_hi, hi_e, FJ), (f_lo, lo_e, FJ), (f_s, src_e, FJ), (f_d, dst_e, FJ),
                          (g_f, gdst, GJ), (gs_f, gsrc, GJ)):
            for k in range(0, n, 4):
                m = min(4, n - k)
                turned.append((of[:, k:k + m, :], to[:, k * P:(k + m) * P], m))
        n_router = 4 * FJ // 4

        s_fd = sem("s_fd")
        s_gd = sem("s_gd")
        s_ff = sem("s_ff")
        s_gf = sem("s_gf")
        s_tr = sem("s_tr")
        s_trc = sem("s_trc")
        s_hist = sem("s_hist")
        s_histm = sem("s_histm")
        s_base = sem("s_base")
        s_basev = sem("s_basev")
        s_cr = sem("s_cr")
        s_crb = sem("s_crb")
        s_gp = sem("s_gp")
        s_gpm = sem("s_gpm")
        s_hirow = sem("s_hirow")
        s_pad = sem("s_pad")

        with nc.Block() as block:
            @block.sync
            def _(sp):
                FULL = EG // (P * P) * P * P
                left = EG - FULL
                rows = left // P
                sp.wait_ge(s_v, 1)
                for t_i, a in ((gd_i, dst), (gs_i, src)):
                    sp.dma_start(t_i[:, 0:GJ - 1, :], a[0:FULL].rearrange("(j p e) -> p j e", p=P, e=P)).then_inc(s_gd, 16)
                    sp.dma_start(t_i[0:rows, GJ - 1, :], a[FULL:FULL + rows * P].rearrange("(p e) -> p e", e=P)).then_inc(s_gd, 16)
                    sp.dma_start(t_i[rows:rows + 1, GJ - 1, 0:left - rows * P],
                                 a[FULL + rows * P:EG].rearrange("(p e) -> p e", p=1)).then_inc(s_gd, 16)
                for t_i, k in ((fd_i, 1), (fs_i, 0)):
                    sp.dma_start(t_i, fedge[k, :].rearrange("(j p e) -> p j e", p=P, e=P)).then_inc(s_fd, 16)
                sp.dma_start(wkv, wkv_t.rearrange("(k p) f -> p k f", p=P)).then_inc(s_w, 16)
                sp.dma_start(wq, wqkv[0:INNER, :].rearrange("(k p) f -> p k f", p=P)).then_inc(s_w, 16)
                sp.dma_start(wo, wout_t.rearrange("(k p) f -> p k f", p=P)).then_inc(s_w, 16)
                sp.dma_start(wg[:], gnn_w.rearrange("(k p) f -> p k f", p=P)).then_inc(s_w, 16)
                sp.dma_start(wr[:, :, 0:16], w_gat.rearrange("(k p) f -> p k f", p=P)).then_inc(s_w, 16)
                sp.dma_start(att[:, 0, :], to_all(att_src.rearrange("(o h) e -> o (h e)", o=1))).then_inc(s_w, 16)
                sp.dma_start(att[:, 1, :], to_all(att_dst.rearrange("(o h) e -> o (h e)", o=1))).then_inc(s_w, 16)
                sp.dma_start(bias_x[:], to_all(gnn_b.rearrange("(o f) -> o f", o=1))).then_inc(s_w, 16)
                sp.dma_start(bout_b[:], to_all(bout.rearrange("(o f) -> o f", o=1))).then_inc(s_w, 16)
                sp.wait_ge(s_ff, 1)
                sp.dma_start(hi_rows.rearrange("(j p) e -> p j e", p=P), f_hib).then_inc(s_hirow, 16)
                sp.wait_ge(s_gf, 1)
                sp.dma_start(chunk_lo.rearrange("(p j) o -> p (j o)", p=P), small[:, 0:GJ]).then_inc(s_cr, 16)
                sp.dma_start(chunk_hi.rearrange("(p j) o -> p (j o)", p=P), small[:, 16:16 + GJ]).then_inc(s_cr, 16)
                sp.wait_ge(s_cr, 32)
                sp.dma_start(lo_b, to_all(chunk_lo.rearrange("c o -> o c"))).then_inc(s_crb, 16)
                sp.dma_start(hi_b, to_all(chunk_hi.rearrange("c o -> o c"))).then_inc(s_crb, 16)
                sp.wait_ge(s_hirow, 16)

            @block.gpsimd
            def _(pool):
                nc.gpsimd.memset(ident[:], 0.0)
                nc.gpsimd.memset(below[:], 1.0)
                nc.gpsimd.memset(above[:], 1.0)
                nc.gpsimd.iota(iota_j[:], [[1, P]], base=0, channel_multiplier=0, allow_small_or_imprecise_dtypes=True)
                nc.gpsimd.iota(iota_p[:], [[0, 1]], base=0, channel_multiplier=1, allow_small_or_imprecise_dtypes=True)
                nc.gpsimd.iota(neg_first[:], [[-NP, NT]], base=0, channel_multiplier=0, allow_small_or_imprecise_dtypes=True)
                nc.gpsimd.iota(pad_list[:], [[0, BLK]], base=N, channel_multiplier=0).then_inc(s_const, 1)
                pool.wait_ge(s_const, 1)
                nc.gpsimd.affine_select(out=ident[:], in_=ident[:], compare_op=ALU.not_equal, fill=1.0, base=0,
                                        pattern=[[-1, P]], channel_multiplier=1)
                nc.gpsimd.affine_select(out=below[:], in_=below[:], compare_op=ALU.is_gt, fill=0.0, base=0,
                                        pattern=[[-1, P]], channel_multiplier=1)
                nc.gpsimd.affine_select(out=above[:], in_=above[:], compare_op=ALU.is_gt, fill=0.0, base=0,
                                        pattern=[[1, P]], channel_multiplier=-1).then_inc(s_const, 1)

            @block.vector
            def _(dve):
                v = nc.vector
                v.memset(gd_i[:, GJ - 1, :], 16000)
                v.memset(gs_i[:, GJ - 1, :], 0).then_inc(s_v, 1)
                v.memset(zeros_b[:], 0.0)
                v.memset(eps_c[:], EPS).then_inc(s_v, 1)

                def tile_of(dst_f, hi, tmp):
                    v.tensor_scalar(tmp, dst_f, 1.0 / NP, 0.5 / NP - 0.5, ALU.mult, ALU.add)
                    v.drain()
                    v.tensor_scalar(hi, tmp, MAGIC, MAGIC, ALU.add, ALU.subtract)
                    v.drain()

                dve.wait_ge(s_fd, 32)
                v.tensor_copy(f_d, fd_i)
                v.tensor_copy(f_s, fs_i)
                v.drain()
                tile_of(f_d, f_hi, f_lo)
                v.tensor_copy(f_hib, f_hi)
                v.scalar_tensor_tensor(out=f_lo, in0=f_hi, scalar=-float(NP), in1=f_d, op0=ALU.mult, op1=ALU.add)
                v.drain()
                v.memset(small[:, 60:61], 0.0).then_inc(s_ff, 1)
                def copy_out(first, last):
                    for k in range(first, last):
                        _, to, n = turned[k]
                        dve.wait_ge(s_tr, k + 1)
                        v.tensor_copy(to, PS[k % 2][:, 0:n * P]).then_inc(s_trc, 1)

                copy_out(0, n_router)
                dve.wait_ge(s_gd, 96)
                v.tensor_copy(g_f, gd_i)
                v.tensor_copy(gs_f, gs_i)
                v.drain()
                tile_of(g_f, gh, gt)
                v.tensor_reduce(small[:, 0:GJ], gh, AX.X, ALU.min)
                v.tensor_reduce(small[:, 16:16 + GJ], gh, AX.X, ALU.max)
                v.drain()
                v.memset(small[:, 61:62], 0.0).then_inc(s_gf, 1)
                copy_out(n_router, len(turned))
                dve.wait_ge(s_crb, 32)
                dve.wait_ge(s_gp, 1)
                v.tensor_scalar(m_b, lo_b, iota_p[:], None, ALU.is_le)
                v.drain()
                v.scalar_tensor_tensor(out=cand, in0=hi_b, scalar=iota_p[:], in1=m_b, op0=ALU.is_ge, op1=ALU.mult)
                v.drain()
                v.scalar_tensor_tensor(out=m_b, in0=chunk_no, scalar=-4096.0, in1=cand, op0=ALU.add, op1=ALU.mult)
                v.scalar_tensor_tensor(out=lo_b, in0=chunk_no, scalar=1.0, in1=cand, op0=ALU.add, op1=ALU.mult)
                v.drain()
                v.tensor_reduce(small[:, 40:41], m_b, AX.X, ALU.min)
                v.tensor_reduce(small[:, 41:42], lo_b, AX.X, ALU.max)
                v.drain()
                v.tensor_scalar(small[:, 42:43], small[:, 40:41], 4096.0, None, ALU.add)
                v.drain()
                v.tensor_tensor(small[:, 43:44], small[:, 41:42], small[:, 42:43], ALU.subtract)
                v.tensor_scalar(small[:, 44:45], small[:, 42:43], float(GC), None, ALU.min)
                v.drain()
                v.tensor_scalar(small[:, 45:46], small[:, 43:44], 0.0, None, ALU.max)
                v.drain()
                v.tensor_scalar(small[:, 46:47], small[:, 45:46], 1.0 / GU, (GU - 1) / (2.0 * GU), ALU.mult, ALU.add)
                v.drain()
                v.tensor_scalar(small[:, 45:46], small[:, 46:47], MAGIC, MAGIC, ALU.add, ALU.subtract)
                v.drain()
                v.memset(small[:, 63:64], 0.0).then_inc(s_gpm, 1)
                dve.wait_ge(s_gp, 2)
                v.tensor_copy(gplan[:, :], SM[0:1, 0:3 * NT])
                v.memset(gdst[:, GC:GW], FAR)
                v.memset(gsrc[:, GC:GW], 0)
                dve.wait_ge(s_w, 9 * 16)
                heads = wkv.rearrange("p k (h e) -> p (k h) e", e=DH)
                v.tensor_reduce(small[:, 0:32], heads, AX.X, ALU.add)
                v.drain()
                v.tensor_scalar(small[:, 0:32], small[:, 0:32], 1.0 / DH, None, ALU.mult)
                v.drain()
                v.tensor_tensor(heads, heads, along(small[:, 0:32], DH), ALU.subtract)
                v.tensor_tensor(bias_x[:], bias_x[:], bout_b[:], ALU.add)
                v.drain()
                for k in range(2):
                    for side in range(2):
                        v.tensor_tensor(small[:, 0:16], wr[:, k, 0:16], att[:, side, :], ALU.mult)
                        v.drain()
                        v.tensor_reduce(wr[:, k, 16 + 4 * side:20 + 4 * side],
                                        small[:, 0:16].rearrange("p (h e) -> p h e", e=4), AX.X, ALU.add)
                        v.drain()

            @block.tensor
            def _(pe):
                pe.wait_ge(s_const, 2)
                pe.wait_ge(s_ff, 1)
                for k, (of, _, n) in enumerate(turned):
                    if k == n_router:
                        pe.wait_ge(s_gf, 1)
                    if k >= 2:
                        pe.wait_ge(s_trc, k - 1)
                    for q in range(n):
                        last = nc.tensor.transpose(PS[k % 2][:, q * P:(q + 1) * P], of[:, q, :], ident[:])
                    last.then_inc(s_tr, 1)
                pe.wait_ge(s_gpm, 1)
                c0, ng = small[0:NT, 44:45], small[0:NT, 45:46]
                nc.tensor.matmul(SM[0:1, 0:NT], c0, ident[0:NT, 0:NT], start=True, stop=True)
                nc.tensor.matmul(SM[0:1, NT:2 * NT], ng, ident[0:NT, 0:NT], start=True, stop=True)
                nc.tensor.matmul(SM[0:1, 2 * NT:3 * NT], ng, above[0:NT, 0:NT], start=True, stop=True).then_inc(s_gp, 1)

            @block.scalar
            def _(act):
                act.wait_ge(s_const, 2)
                for j in range(GJ):
                    nc.scalar.activation(chunk_no.rearrange("q (p j) -> q j p", j=GJ)[:, j, :], iota_j[:], ACT.Copy, bias=float(j * P))
                act.drain()
                act.sem_inc(s_gp, 1)
        setup.close()
        if dbg is not None and dbg.get("stop") == "setup":
            return dump(nc, dbg, dict(gplan=gplan, gsrc=gsrc, gdst=gdst, hi_e=hi_e, lo_e=lo_e, src_e=src_e,
                                      wr=wr, wkv=wkv))

        with ExitStack() as stage, nc.Block() as block:
            two = lambda name, shape, dt=f32: [stage.enter_context(nc.sbuf_tensor(f"{name}{u}", shape, dt)) for u in range(2)]
            ev = lambda name: stage.enter_context(nc.semaphore(name))
            x_in, x_n = two("x_in", [NP, D]), two("x_n", [NP, D])
            st6, mv, rstd = two("st6", [NP, 6]), two("mv", [NP, 2]), two("rstd", [NP, 1])
            k_sb, v_sb, sq = two("k_sb", [NP, INNER]), two("v_sb", [NP, INNER]), two("sq", [NP, 2, INNER])
            ss, rr = two("ss", [NP, 16]), two("rr", [NP, 8])
            x_t = two("x_t", [P, 2 * NP])
            XT, KP, VP, DT = PS[0:2], PS[4:6], PS[6:8], PS[3]
            s_xl = [ev(f"s_xl{u}") for u in range(2)]
            s_xs = [ev(f"s_xs{u}") for u in range(2)]
            s_ts = [ev(f"s_ts{u}") for u in range(2)]
            s_var = ev("s_var")
            s_std = ev("s_std")
            s_xn = ev("s_xn")
            s_turn = ev("s_turn")
            s_turnc = ev("s_turnc")
            s_kv = ev("s_kv")
            s_sq = ev("s_sq")
            s_ss = ev("s_ss")
            s_rt = ev("s_rt")
            s_vn = ev("s_vn")
            s_dt = ev("s_dt")
            s_oh = ev("s_oh")
            s_ohm = ev("s_ohm")

            @block.sync
            def _(sp):
                def load(t, u):
                    sp.wait_ge(s_xn, t + 1)
                    sp.dma_start(x_in[u][:], x[bass.ds(t * NP, NP), :]).then_inc(s_xl[u], 16)

                def store(t, u):
                    sp.wait_ge(s_xn, t + 3)
                    sp.dma_start(xn_rows[bass.ds(t * NP, NP), :], x_n[u][:]).then_inc(s_xs[u], 16)

                def store_turned(t, u):
                    sp.wait_ge(s_turnc, t + 3)
                    sp.dma_start(xn_turned[bass.ds(t, 1), :, :].rearrange("o p c -> p (o c)"), x_t[u][:]).then_inc(s_ts[u], 16)

                steps(sp, NT, 2, [(0, load), (1, store), (2, store_turned)])
                for u in range(2):
                    sp.wait_ge(s_ts[u], 16 * NT // 2)
                    sp.wait_ge(s_xs[u], 16 * NT // 2)

            def hist(dve, i):
                v = nc.vector
                for h in range(2):
                    dve.wait_ge(s_ohm, i * 2 + (h + 1))
                    for to, of, n in ((oh_hi, hi_e, NT), (oh_lo, lo_e, NP)):
                        last = v.tensor_tensor(to[:, 4 * h:4 * h + 4, :],
                                               iota_j[:, 0:n].rearrange("p (o n) -> p o n", o=1).broadcast_to([P, 4, n]),
                                               along(of[:, bass.ds(i * 8 + 4 * h, 4)], n), ALU.is_equal)
                    last.then_inc(s_oh, 1)

            @block.vector
            def _(dve):
                v = nc.vector
                dve.sem_inc(s_xn, 2)
                dve.sem_inc(s_vn, 2)

                def norm(t, u):
                    dve.wait_ge(s_xl[u], (t - u) * 8 + 16)
                    v.bn_stats(st6[u][:], x_in[u][:])
                    v.drain()
                    v.bn_aggr(mv[u][:], st6[u][:]).then_inc(s_var, 1)
                    dve.wait_ge(s_std, t + 1)
                    v.reciprocal(rstd[u][:], rstd[u][:])
                    v.drain()
                    wait_after(dve, s_xs[u], (t - u) * 8)
                    v.tensor_scalar(x_n[u][:], x_in[u][:], mv[u][:, 0:1], rstd[u][:], ALU.subtract, ALU.mult).then_inc(s_xn, 1)

                def values(t, u):
                    dve.wait_ge(s_sq, t + 1)
                    v.tensor_reduce(ss[u][:], sq[u][:].rearrange("p s (h e) -> p (s h) e", e=DH), AX.X, ALU.add).then_inc(s_ss, 1)
                    dve.wait_ge(s_rt, t + 1)
                    v.reciprocal(ss[u][:], ss[u][:])
                    v.drain()
                    v.tensor_tensor(rr[u][:], ss[u][:, 0:8], ss[u][:, 8:16], ALU.mult)
                    v.drain()
                    dve.wait_ge(s_dt, t + 1)
                    v.tensor_tensor(v_sb[u][:].rearrange("p (h e) -> p h e", e=DH),
                                    VP[u][0:NP, :].rearrange("p (h e) -> p h e", e=DH), along(rr[u][:], DH),
                                    ALU.mult).then_inc(s_vn, 1)

                steps(dve, NT, 2, [(2, values), (0, norm), (0, lambda t, u: hist(dve, t))])
                with dve.Fori(NT, FC // 8) as i:
                    hist(dve, i)

            @block.scalar
            def _(act):
                a = nc.scalar.activation
                act.sem_inc(s_turnc, 2)

                def std(t, u):
                    act.wait_ge(s_var, t + 1)
                    a(rstd[u][:], mv[u][:, 1:2], ACT.Sqrt, bias=eps_c[0:NP, :]).then_inc(s_std, 1)

                def turn_copy(t, u):
                    act.wait_ge(s_turn, t + 1)
                    wait_after(act, s_ts[u], (t - u) * 8)
                    a(x_t[u][:], XT[u][:, 0:2 * NP], ACT.Copy).then_inc(s_turnc, 1)

                def squares(t, u):
                    act.wait_ge(s_kv, t + 1)
                    act.wait_ge(s_dt, t + 1)
                    a(k_sb[u][:], KP[u][0:NP, :], ACT.Copy)
                    a(sq[u][:, 0, :], KP[u][0:NP, :], ACT.Square)
                    a(sq[u][:, 1, :], VP[u][0:NP, :], ACT.Square).then_inc(s_sq, 1)
                    act.wait_ge(s_ss, t + 1)
                    a(ss[u][:], ss[u][:], ACT.Sqrt, bias=eps_c[0:NP, :], scale=1.0 / DH).then_inc(s_rt, 1)

                steps(act, NT, 2, [(2, squares), (1, turn_copy), (0, std)])

            def count(pe, i):
                for h in range(2):
                    pe.wait_ge(s_oh, i * 2 + (h + 1))
                    for q in range(4 * h, 4 * h + 4):
                        last = nc.tensor.matmul(CNT[0:NT, 0:NP], oh_hi[:, q, :], oh_lo[:, q, :], start=False, stop=False)
                    last.then_inc(s_ohm, 1)

            @block.tensor
            def _(pe):
                mm = nc.tensor.matmul
                zero = lambda to, m, n, **kw: mm(to, zeros_b[:, 0:m], zeros_b[:, 0:n], **kw)
                zero(CNT[0:NT, 0:NP], NT, NP, start=True, stop=False)
                zero(DT[:, :], P, 512, start=True, stop=False)
                pe.sem_inc(s_ohm, 2)
                pe.sem_inc(s_dt, 2)

                def turn(t, u):
                    pe.wait_ge(s_xn, t + 3)
                    pe.wait_ge(s_turnc, t + 1)
                    for k in range(2):
                        last = nc.tensor.transpose(XT[u][:, k * NP:(k + 1) * NP], x_n[u][:, k * P:(k + 1) * P],
                                                   ident[0:NP, 0:NP])
                    last.then_inc(s_turn, 1)

                def keys_values(t, u):
                    pe.wait_ge(s_turnc, t + 3)
                    pe.wait_ge(s_vn, t + 1)
                    for k in range(2):
                        mm(KP[u][0:NP, :], x_t[u][:, k * NP:(k + 1) * NP], wkv[:, k, 0:INNER], start=k == 0, stop=k == 1)
                    for k in range(2):
                        last = mm(VP[u][0:NP, :], x_t[u][:, k * NP:(k + 1) * NP], wkv[:, k, INNER:2 * INNER],
                                  start=k == 0, stop=k == 1)
                    last.then_inc(s_kv, 1)

                def outer(t, u):
                    pe.wait_ge(s_vn, t + 3)
                    for q in range(4):
                        last = mm(DT[:, q * P:(q + 1) * P], v_sb[u][:, q * P:(q + 1) * P], k_sb[u][:, q * P:(q + 1) * P],
                                  start=False, stop=False)
                    last.then_inc(s_dt, 1)

                steps(pe, NT, 2, [(3, outer), (2, keys_values), (1, turn), (0, lambda t, u: count(pe, t))])
                with pe.Fori(NT, FC // 8) as i:
                    count(pe, i)
                zero(CNT[0:NT, 0:NP], NT, NP, start=False, stop=True)
                zero(DT[:, :], P, 512, start=False, stop=True)

        with ExitStack() as stage, nc.Block() as block:
            ev = lambda name: stage.enter_context(nc.semaphore(name))
            dt_sb = stage.enter_context(nc.sbuf_tensor("dt_sb", [P, 4, P], f32))
            u_sb = stage.enter_context(nc.sbuf_tensor("u_sb", [P, 4, D], f32))
            LOOK, UP, MP = PS[0:2], PS[4:6], PS[6]
            s_nb = ev("s_nb")
            s_plan = ev("s_plan")
            s_plan_sb = ev("s_plan_sb")
            s_fill = ev("s_fill")
            s_filled = ev("s_filled")
            s_dts = ev("s_dts")
            s_u = ev("s_u")
            s_uc = ev("s_uc")
            s_m = ev("s_m")
            s_bl = [ev(f"s_bl{h}") for h in range(2)]
            s_blf = ev("s_blf")
            s_oht = ev("s_oht")
            s_oh = ev("s_oh2")
            s_t = ev("s_t")
            s_look = ev("s_look")
            s_cnt = ev("s_cnt")
            s_sel = ev("s_sel")
            s_pos = ev("s_pos")
            s_put = [ev(f"s_put{q}") for q in range(8)]

            @block.sync
            def _(sp):
                sp.wait_ge(s_plan_sb, 1)
                rounds = sp.value_load(fplan[0:1, 2 * NT:2 * NT + 1], min_val=0, max_val=LIST_BLOCKS // P)
                def one_round(b):
                    sp.dma_start(lists[bass.ds(b * (P * BLK), P * BLK), :].rearrange("(p e) o -> p (e o)", p=P),
                                 pad_list[:]).then_inc(s_fill, 16)
                    sp.wait_ge(s_fill, b * 16 + 16)
                    sp.sem_inc(s_gate, 1)
                repeat(sp, rounds, one_round)
                sp.sem_inc(s_filled, 1)
                with sp.Fori(0, FC // 8) as i:
                    for h in range(2):
                        sp.wait_ge(s_blf, i * 2 + (h + 1))
                        c = i * 8 + 4 * h
                        sp.dma_start(dst_b[h][:], to_all(fedge[1:2, bass.ds(c * P, 4 * P)])).then_inc(s_bl[h], 16)
                        sp.dma_start(hi_bc[h][:], to_all(hi_rows[bass.ds(c, 4), :].rearrange("(o c) e -> o (c e)", o=1))).then_inc(s_bl[h], 16)

            @block.gpsimd
            def _(pool):
                pool.wait_ge(s_filled, 1)
                with pool.Fori(0, FC // 8) as i:
                    for h in range(2):
                        pool.wait_ge(s_pos, i * 2 + (h + 1))
                        pool.sem_inc(s_gate, 1)
                        for q in range(4 * h, 4 * h + 4):
                            pool.indirect_dma_start(
                                out=lists, out_offset=bass.IndirectOffsetOnAxis(ap=pos_i[:, q:q + 1], axis=0),
                                in_=val_i[:, q:q + 1], in_offset=None).then_inc(s_put[q], 16)
                for q in range(8):
                    pool.wait_ge(s_put[q], 16 * FC // 8)

            @block.vector
            def _(dve):
                v = nc.vector
                v.tensor_reduce(small[0:NT, 32:33], CNT[0:NT, 0:NP], AX.X, ALU.max)
                v.drain()
                v.tensor_scalar(small[0:NT, 33:34], small[0:NT, 32:33], 1.0 / FU, (FU - 1) / (2.0 * FU), ALU.mult, ALU.add)
                v.drain()
                v.tensor_scalar(small[0:NT, 34:35], small[0:NT, 33:34], MAGIC, MAGIC, ALU.add, ALU.subtract).then_inc(s_nb, 1)
                dve.wait_ge(s_plan, 1)
                v.tensor_scalar(base8[0:NT, :], UP[0][0:NT, 256:257], float(FU), None, ALU.mult)
                v.tensor_copy(fplan[0:1, 0:2 * NT], UP[0][0:1, 0:2 * NT])
                v.tensor_scalar(small[0:1, 36:37], UP[0][0:1, 260:261], 1.0 / P, (P - 1) / (2.0 * P), ALU.mult, ALU.add)
                v.drain()
                v.tensor_scalar(small[0:1, 37:38], small[0:1, 36:37], MAGIC, MAGIC, ALU.add, ALU.subtract)
                v.drain()
                v.tensor_copy(fplan[0:1, 2 * NT:2 * NT + 1], small[0:1, 37:38]).then_inc(s_plan_sb, 1)
                v.memset(dt_sb[:], 0.0)
                v.drain()
                for lo in (0, DH):
                    last = v.tensor_scalar(dt_sb[lo:lo + DH, :, lo:lo + DH],
                                           PS[3][lo:lo + DH, :].rearrange("p (q d) -> p q d", q=4)[:, :, lo:lo + DH],
                                           1.0 / N, None, ALU.mult)
                last.then_inc(s_dts, 1)
                for q in range(2):
                    dve.wait_ge(s_u, q + 1)
                    v.tensor_copy(u_sb[:, 2 * q:2 * q + 2, :], UP[q][:, :].rearrange("p (q f) -> p q f", q=2)).then_inc(s_uc, 1)
                dve.wait_ge(s_m, 1)
                v.tensor_copy(mix[:], MP[:, :].rearrange("p (k f) -> p k f", k=2))

                dve.sem_inc(s_blf, 2)
                dve.sem_inc(s_sel, 2)
                def place(i):
                    for h in range(2):
                        dve.wait_ge(s_bl[h], i * 32 + 32)
                        v.tensor_scalar(oh_t[h][:], hi_bc[h][0:NT, :], iota_p[0:NT, :], None, ALU.is_equal).then_inc(s_oht, 1)
                        cols = bass.ds(i * 8 + 4 * h, 4)
                        for to, of, n in ((oh_hi, hi_e, NT), (oh_lo, lo_e, NP)):
                            last = v.tensor_tensor(to[:, 4 * h:4 * h + 4, :],
                                                   iota_j[:, 0:n].rearrange("p (o n) -> p o n", o=1).broadcast_to([P, 4, n]),
                                                   along(of[:, cols], n), ALU.is_equal)
                        last.then_inc(s_oh, 1)
                        for q in range(4 * h, 4 * h + 4):
                            e = (q % 4) * P
                            last = v.scalar_tensor_tensor(out=junk[:, q, :], in0=dst_b[h][:, e:e + P], scalar=dst_e[:, bass.ds(i * 8 + q, 1)],
                                                          in1=below[:], op0=ALU.is_equal, op1=ALU.mult, accum_out=rk[:, q:q + 1])
                        last.then_inc(s_blf, 1)
                        for q in range(4 * h, 4 * h + 4):
                            dve.wait_ge(s_look, i * 8 + (q + 1))
                            v.scalar_tensor_tensor(out=junk_l[:, q, 0:NP], in0=iota_j[:, 0:NP], scalar=lo_e[:, bass.ds(i * 8 + q, 1)],
                                                   in1=LOOK[q % 2][:, 0:NP], op0=ALU.is_equal, op1=ALU.mult,
                                                   accum_out=tv[:, q:q + 1]).then_inc(s_sel, 1)
                        v.drain()
                        s4 = slice(4 * h, 4 * h + 4)
                        v.tensor_tensor(tv[:, s4], tv[:, s4], rk[:, s4], ALU.add)
                        v.drain()
                        v.tensor_scalar(blk_f[:, s4], tv[:, s4], 1.0 / FU, -(FU - 1) / (2.0 * FU), ALU.mult, ALU.add)
                        v.scalar_tensor_tensor(out=pos_f[:, s4], in0=lo_e[:, cols], scalar=float(FU), in1=tv[:, s4], op0=ALU.mult, op1=ALU.add)
                        v.drain()
                        v.tensor_scalar(blk_f[:, s4], blk_f[:, s4], MAGIC, MAGIC, ALU.add, ALU.subtract)
                        v.drain()
                        for q in range(4 * h, 4 * h + 4):
                            wait_after(dve, s_put[q], i * 16)
                        v.scalar_tensor_tensor(out=pos_i[:, s4], in0=blk_f[:, s4], scalar=float(BLK - FU), in1=pos_f[:, s4], op0=ALU.mult, op1=ALU.add)
                        v.tensor_copy(val_i[:, s4], src_e[:, cols]).then_inc(s_pos, 1)

                place(0)
                with dve.Fori(1, FC // 8) as i:
                    place(i)

            @block.scalar
            def _(act):
                a = nc.scalar.activation
                act.wait_ge(s_plan_sb, 1)
                a(t_sb[:], CNT[0:NT, 0:NP], ACT.Identity, bias=base8[0:NT, :], scale=0.0).then_inc(s_t, 1)
                with act.Fori(0, FC) as c:
                    act.wait_ge(s_cnt, c + 1)
                    a(t_sb[:], CNT[0:NT, 0:NP], ACT.Identity, bias=base8[0:NT, :]).then_inc(s_t, 1)

            @block.tensor
            def _(pe):
                mm = nc.tensor.matmul
                pe.wait_ge(s_nb, 1)
                nb = small[0:NT, 34:35]
                mm(UP[0][0:1, 0:NT], nb, ident[0:NT, 0:NT], start=True, stop=True)
                mm(UP[0][0:1, NT:2 * NT], nb, above[0:NT, 0:NT], start=True, stop=True)
                mm(UP[0][0:1, 260:261], nb, above[0:NT, NT:NT + 1], start=True, stop=True)
                mm(UP[0][0:NT, 256:257], above[0:NT, 0:NT], nb, start=True, stop=True).then_inc(s_plan, 1)
                pe.wait_ge(s_dts, 1)
                for q in range(4):
                    last = mm(UP[q // 2][:, (q % 2) * D:(q % 2 + 1) * D], dt_sb[:, q, :], wo[:, q, :], start=True, stop=True)
                    if q % 2:
                        last.then_inc(s_u, 1)
                pe.wait_ge(s_uc, 2)
                for k in range(2):
                    for q in range(4):
                        last = mm(MP[:, k * D:(k + 1) * D], wq[:, q, k * P:(k + 1) * P], u_sb[:, q, :], start=q == 0, stop=q == 3)
                last.then_inc(s_m, 1)

                pe.wait_ge(s_t, 1)
                mm(CNT[0:NT, 0:NP], zeros_b[:, 0:NT], zeros_b[:, 0:NP], start=True, stop=True)
                with pe.Fori(0, FC // 8) as i:
                    for h in range(2):
                        pe.wait_ge(s_oht, i * 2 + (h + 1))
                        pe.wait_ge(s_oh, i * 2 + (h + 1))
                        for q in range(4 * h, 4 * h + 4):
                            c = i * 8 + (q + 1)
                            pe.wait_ge(s_sel, c)
                            pe.wait_ge(s_t, c)
                            mm(LOOK[q % 2][:, 0:NP], oh_t[h][:, (q % 4) * P:(q % 4 + 1) * P], t_sb[:], start=True, stop=True).then_inc(s_look, 1)
                            mm(CNT[0:NT, 0:NP], oh_hi[:, q, :], oh_lo[:, q, :], start=False, stop=True, skip_group_check=True).then_inc(s_cnt, 1)
        if dbg is not None and dbg.get("stop") == "place":
            return dump(nc, dbg, dict(fplan=fplan, mix=mix, xt=xn_turned, lists=lists[0:384 * BLK, :].rearrange("(b n) o -> b (n o)", b=384)))

        with ExitStack() as stage, nc.Block() as block:
            one = lambda name, shape, dt=f32: stage.enter_context(nc.sbuf_tensor(name, shape, dt))
            two = lambda name, shape, dt=f32: [one(f"{name}{u}", shape, dt) for u in range(2)]
            ev = lambda name: stage.enter_context(nc.semaphore(name))
            rows = one("rows", [P, GU, D + 1])
            oh = one("oh", [P, GU, NP])
            idx = one("idx", [P, GU], i32)
            s_sb, s_t, x_t, x_in = two("s_sb", [NP, D]), two("s_t", [P, 2 * NP]), two("x_tc", [P, 2 * NP]), two("x_inc", [NP, D])
            rdeg, ssq, rstd = two("rdeg", [NP, 1]), two("ssq", [NP, 1]), two("rstdc", [NP, 1])
            sq = two("sqc", [NP, D])
            x1, x2, x2_t = two("x1", [NP, D]), two("x2", [NP, D]), two("x2_t", [P, 2 * NP])
            st6, mv, rt = two("st6c", [NP, 6]), two("mvc", [NP, 2]), two("rt", [NP, ROW])
            pad_row = one("pad_row", [1, ROW])
            SUM, ST, G, MX, X2, H = PS[0:2], PS[2], PS[3], PS[4], PS[5], PS[6]
            s_ini = ev("s_ini")
            s_wl = ev("s_wl")
            s_ix = ev("s_ix")
            s_rows = [ev(f"s_rows{q}") for q in range(GU)]
            s_ohr = ev("s_ohr")
            s_used = ev("s_used")
            s_sum = ev("s_sum")
            s_mean = ev("s_mean")
            s_st = ev("s_st")
            s_stc = ev("s_stc")
            s_xl = [ev(f"s_xlc{u}") for u in range(2)]
            s_lin = ev("s_lin")
            s_nrm = ev("s_nrm")
            s_x1 = ev("s_x1")
            s_std = ev("s_stdc")
            s_x2 = ev("s_x2")
            s_x2p = ev("s_x2p")
            s_x2c = ev("s_x2c")
            s_h = ev("s_h")
            s_hc = ev("s_hc")
            s_x1s = [ev(f"s_x1s{u}") for u in range(2)]
            s_x2s = [ev(f"s_x2s{u}") for u in range(2)]
            s_rts = [ev(f"s_rts{u}") for u in range(2)]
            s_pr = ev("s_pr")

            def first_chunk(c):
                return nc.s_assert_within(c, 0, GC, skip_runtime_bounds_check_because=
                                          "a tile's rounds end at most GU - 1 chunks past its last chunk")

            def plan(eng, t):
                return (eng.value_load(gplan[0:1, bass.ds(t, 1)], min_val=0, max_val=GC - 1),
                        eng.value_load(gplan[0:1, bass.ds(t + NT, 1)], min_val=0, max_val=GC // GU + 1),
                        eng.value_load(gplan[0:1, bass.ds(t + 2 * NT, 1)], min_val=0, max_val=NT * (GC // GU + 1)))

            @block.sync
            def _(sp):
                for e in range(NE):
                    sp.dma_start(w1_sb[:, :, e, :], w1[e].rearrange("(k p) f -> p k f", p=P)).then_inc(s_wl, 16)
                    sp.dma_start(w2_sb[:, e, :, :], w2[e].rearrange("(k p) f -> p k f", p=P)).then_inc(s_wl, 16)
                sp.wait_ge(s_ini, 1)
                sp.dma_start(route_rows[N:N + 1, :], pad_row[:]).then_inc(s_pr, 16)

                def load(t, u):
                    sp.wait_ge(s_x2, t + 1)
                    sp.dma_start(x_in[u][:], x[bass.ds(t * NP, NP), :]).then_inc(s_xl[u], 16)
                    sp.dma_start(x_t[u][:], xn_turned[bass.ds(t, 1), :, :].rearrange("o p c -> p (o c)")).then_inc(s_xl[u], 16)

                def store_x1(t, u):
                    sp.wait_ge(s_x2, t + 3)
                    sp.dma_start(x1_rows[bass.ds(t * NP, NP), :], x1[u][:]).then_inc(s_x1s[u], 16)

                def store_x2(t, u):
                    sp.wait_ge(s_x2c, t + 2)
                    sp.dma_start(x2_turned[bass.ds(t, 1), :, :].rearrange("o p c -> p (o c)"), x2_t[u][:]).then_inc(s_x2s[u], 16)

                def store_rt(t, u):
                    sp.wait_ge(s_hc, t + 2)
                    sp.dma_start(route_rows[bass.ds(t * NP, NP), :], rt[u][:]).then_inc(s_rts[u], 16)

                steps(sp, NT, 2, [(1, load), (3, store_x1), (3, store_x2), (4, store_rt)])
                for u in range(2):
                    for s in (s_x1s, s_x2s, s_rts):
                        sp.wait_ge(s[u], 16 * NT // 2)
                sp.wait_ge(s_pr, 16)
                sp.wait_ge(s_wl, 2 * NE * 16)

            @block.gpsimd
            def _(pool):
                def gather(t, u):
                    c0, rounds, before = plan(pool, t)
                    def one_round(g):
                        k = g + before
                        c = first_chunk(c0 + g * GU)
                        for q in range(0, GU, 3):
                            pool.wait_ge(s_used, k * GU + (q + 3))
                            pool.sem_inc(s_gate, 1)
                            nc.gpsimd.tensor_copy(idx[:, q:q + 3], gsrc[:, bass.ds(c + q, 3)]).then_inc(s_ix, 1)
                            pool.wait_ge(s_ix, k * 3 + (q // 3 + 1))
                            pool.sem_inc(s_gate, 1)
                            for r in range(q, q + 3):
                                pool.indirect_dma_start(out=rows[:, r, 0:D], out_offset=None, in_=xn_rows,
                                                        in_offset=bass.IndirectOffsetOnAxis(ap=idx[:, r:r + 1], axis=0)
                                                        ).then_inc(s_rows[r], 16)

                    repeat(pool, rounds, one_round)
                with pool.Fori(0, NT) as t:
                    gather(t, 0)

            @block.vector
            def _(dve):
                v = nc.vector
                v.memset(rows[:, :, D:D + 1], 1.0)
                v.memset(pad_row[:, 0:20], 0.0)
                v.memset(pad_row[:, 20:ROW], NEG)
                for u in range(2):
                    v.memset(rt[u][:], 1.0)
                v.drain()
                dve.sem_inc(s_ini, 1)
                dve.sem_inc(s_mean, 2)
                dve.sem_inc(s_x1, 1)
                dve.sem_inc(s_x2, 2)
                dve.sem_inc(s_hc, 1)

                def one_hot(t, u):
                    c0, rounds, before = plan(dve, t)
                    def one_round(g):
                        k = g + before
                        c = first_chunk(c0 + g * GU)
                        for q in range(GU):
                            dve.wait_ge(s_used, k * GU + (q + 1))
                            v.tensor_scalar(oh[:, q, :], iota_j[:, 0:NP], gdst[:, bass.ds(c + q, 1)],
                                            neg_first[:, bass.ds(t, 1)], ALU.subtract, ALU.is_equal).then_inc(s_ohr, 1)

                    repeat(dve, rounds, one_round)
                def mean(t, u):
                    dve.wait_ge(s_sum, t + 1)
                    v.tensor_scalar(rdeg[u][:], SUM[u][0:NP, D:D + 1], 1.0, None, ALU.max)
                    v.drain()
                    v.reciprocal(rdeg[u][:], rdeg[u][:])
                    v.drain()
                    v.tensor_scalar(s_sb[u][:], SUM[u][0:NP, 0:D], rdeg[u][:], None, ALU.mult).then_inc(s_mean, 1)

                def residual(t, u):
                    dve.wait_ge(s_nrm, t + 1)
                    dve.wait_ge(s_xl[u], (t - u) * 16 + 32)
                    wait_after(dve, s_x1s[u], (t - u) * 8)
                    v.reciprocal(ssq[u][:], ssq[u][:])
                    v.drain()
                    v.scalar_tensor_tensor(out=x1[u][:], in0=G[0:NP, 0:D], scalar=ssq[u][:], in1=x_in[u][:], op0=ALU.mult, op1=ALU.add)
                    v.drain()
                    v.tensor_tensor(x1[u][:], x1[u][:], MX[0:NP, 0:D], ALU.add)
                    v.drain()
                    v.tensor_tensor(x1[u][:], x1[u][:], bias_x[0:NP, :], ALU.add)
                    v.drain()
                    v.bn_stats(st6[u][:], x1[u][:])
                    v.drain()
                    v.bn_aggr(mv[u][:], st6[u][:]).then_inc(s_x1, 1)
                    dve.wait_ge(s_std, t + 1)
                    v.reciprocal(rstd[u][:], rstd[u][:])
                    v.drain()
                    v.tensor_scalar(x2[u][:], x1[u][:], mv[u][:, 0:1], rstd[u][:], ALU.subtract, ALU.mult).then_inc(s_x2, 1)

                def router_row(t, u):
                    dve.wait_ge(s_h, t + 1)
                    wait_after(dve, s_rts[u], (t - u) * 8)
                    v.tensor_copy(rt[u][:, 0:20].rearrange("p (h e) -> p h e", e=5)[:, :, 0:4],
                                  H[0:NP, 0:16].rearrange("p (h e) -> p h e", e=4))
                    v.tensor_copy(adst[:, bass.ds(t, 1), :].rearrange("p o h -> p (o h)"), H[0:NP, 20:24])
                    v.tensor_copy(rt[u][:, 20:24], H[0:NP, 16:20]).then_inc(s_hc, 1)

                steps(dve, NT, 2, [(0, one_hot), (1, mean), (4, router_row), (2, residual)])

            @block.scalar
            def _(act):
                a = nc.scalar.activation
                act.sem_inc(s_stc, 1)
                act.sem_inc(s_x2c, 1)

                def turn_mean(t, u):
                    act.wait_ge(s_st, t + 1)
                    a(s_t[u][:], ST[:, 0:2 * NP], ACT.Copy).then_inc(s_stc, 1)

                def norms(t, u):
                    act.wait_ge(s_lin, t + 1)
                    a(sq[u][:], G[0:NP, 0:D], ACT.Square, accum_out=ssq[u][:])
                    act.drain()
                    a(ssq[u][:], ssq[u][:], ACT.Sqrt).then_inc(s_nrm, 1)
                    act.wait_ge(s_x1, t + 2)
                    a(rstd[u][:], mv[u][:, 1:2], ACT.Sqrt, bias=eps_c[0:NP, :]).then_inc(s_std, 1)

                def turn_x2(t, u):
                    act.wait_ge(s_x2p, t + 1)
                    wait_after(act, s_x2s[u], (t - u) * 8)
                    a(x2_t[u][:], X2[:, 0:2 * NP], ACT.Copy).then_inc(s_x2c, 1)

                steps(act, NT, 2, [(1, turn_mean), (2, norms), (3, turn_x2)])

            @block.tensor
            def _(pe):
                mm = nc.tensor.matmul
                pe.sem_inc(s_used, GU)

                def sums(t, u):
                    _, rounds, before = plan(pe, t)
                    pe.wait_ge(s_mean, t + 1)
                    mm(SUM[u][0:NP, 0:D + 1], zeros_b[:, 0:NP], zeros_b[:, 0:D + 1], start=True, stop=False)
                    def one_round(g):
                        k = g + before
                        for q in range(GU):
                            pe.wait_ge(s_rows[q], k * 16 + 16)
                            pe.wait_ge(s_ohr, k * GU + (q + 1))
                            mm(SUM[u][0:NP, 0:D + 1], oh[:, q, :], rows[:, q, :], start=False, stop=False).then_inc(s_used, 1)
                    repeat(pe, rounds, one_round)
                    mm(SUM[u][0:NP, 0:D + 1], zeros_b[:, 0:NP], zeros_b[:, 0:D + 1], start=False, stop=True).then_inc(s_sum, 1)

                def turn_mean(t, u):
                    pe.wait_ge(s_mean, t + 3)
                    pe.wait_ge(s_stc, t + 1)
                    for k in range(2):
                        last = nc.tensor.transpose(ST[:, k * NP:(k + 1) * NP], s_sb[u][:, k * P:(k + 1) * P], ident[0:NP, 0:NP])
                    last.then_inc(s_st, 1)

                def linear(t, u):
                    pe.wait_ge(s_stc, t + 2)
                    pe.wait_ge(s_xl[u], (t - u) * 16 + 32)
                    pe.wait_ge(s_x1, t + 1)
                    for k in range(2):
                        xk = x_t[u][:, k * NP:(k + 1) * NP]
                        mm(G[0:NP, 0:D], xk, wg[:, k, :], start=k == 0, stop=False)
                        mm(G[0:NP, 0:D], s_t[u][:, k * NP:(k + 1) * NP], wg[:, 2 + k, :], start=False, stop=k == 1)
                    for k in range(2):
                        last = mm(MX[0:NP, 0:D], x_t[u][:, k * NP:(k + 1) * NP], mix[:, k, :], start=k == 0, stop=k == 1)
                    last.then_inc(s_lin, 1)

                def turn_x2(t, u):
                    pe.wait_ge(s_x2, t + 3)
                    pe.wait_ge(s_x2c, t + 1)
                    for k in range(2):
                        last = nc.tensor.transpose(X2[:, k * NP:(k + 1) * NP], x2[u][:, k * P:(k + 1) * P], ident[0:NP, 0:NP])
                    last.then_inc(s_x2p, 1)

                def router(t, u):
                    pe.wait_ge(s_x2c, t + 2)
                    pe.wait_ge(s_hc, t + 1)
                    for k in range(2):
                        last = mm(H[0:NP, 0:ROW], x2_t[u][:, k * NP:(k + 1) * NP], wr[:, k, :], start=k == 0, stop=k == 1)
                    last.then_inc(s_h, 1)

                steps(pe, NT, 2, [(0, sums), (4, router), (3, turn_x2), (2, linear), (1, turn_mean)])
        if dbg is not None and dbg.get("stop") == "gnn":
            return dump(nc, dbg, dict(x1=x1_rows, rt=route_rows, adst=adst))

        NG = NT // 4
        with ExitStack() as stage, nc.Block() as block:
            one = lambda name, shape, dt=f32: stage.enter_context(nc.sbuf_tensor(name, shape, dt))
            two = lambda name, shape, dt=f32: [one(f"{name}{u}", shape, dt) for u in range(2)]
            ev = lambda name: stage.enter_context(nc.semaphore(name))
            b1_sb, b2_sb = one("b1_sb", [P, 16]), one("b2_sb", [4, D])
            bg, lg, lb = one("bg", [NP, 16]), one("lg", [NP, 16]), one("lb", [NP, 16])
            first_e = one("first_e", [NP, 4, 4])
            lst = one("lst", [NP, 16, FU], i32)
            ix = one("ix", [NP, FU], i32)
            nb_rows = [one(f"nb_rows{h}", [NP, 5, ROW]) for h in range(2)]
            lk, dif, pr, msg = (one(n, [NP, k, m]) for n, k, m in (("lk", 5, 4), ("dif", 4, 4), ("pr", 4, 4), ("msg", 4, 20)))
            own, ad = one("own", [NP, 4, ROW]), one("ad", [NP, 4])
            res = one("res", [NP, 4, ROW])
            rden, agg, asq = one("rden", [NP, 4, 4]), one("agg", [NP, 4, 16]), one("asq", [NP, 4, 16])
            m4, v4 = one("m4", [NP, 4]), one("v4", [NP, 4])
            sc, sx, gt, eq = one("sc", [NP, 4, 4]), one("sx", [NP, 4, 4]), one("gt", [NP, 4, 4, 4]), one("eq", [NP, 4, 4, 4])
            rank = one("rank", [NP, 4, 4])
            gate = two("gate", [NP, 4, 4])
            gate_t = two("gate_t", [4, 4 * NP])
            x2g = two("x2g", [P, 2, 4, NP])
            hid = two("hid", [P, 16, 4 * NP])
            x1g, acc = two("x1g", [NP, 4, D]), two("acc", [NP, 4, D])
            HP, Y0, Y1, B2, GT = PS[0:2], PS[2:4], PS[4:6], PS[6], PS[7]
            s_pl = ev("s_pl")
            s_fe = ev("s_fe")
            s_ld = ev("s_ld")
            s_lst = ev("s_lst")
            s_lused = ev("s_lused")
            s_ixc = ev("s_ixc")
            s_nb = [ev(f"s_nbr{q}") for q in range(FU)]
            s_half = ev("s_half")
            s_own = [ev(f"s_own{j}") for j in range(4)]
            s_ownf = ev("s_ownf")
            s_dif = ev("s_dif")
            s_pr = ev("s_prob")
            s_var = ev("s_varf")
            s_rt = ev("s_rtf")
            s_ex = ev("s_ex")
            s_exd = ev("s_exd")
            s_gate_r = ev("s_gater")
            s_gt = ev("s_gt")
            s_gtc = ev("s_gtc")
            s_x2l = [ev(f"s_x2l{u}") for u in range(2)]
            s_x1l = [[ev(f"s_x1l{u}{j}") for j in range(4)] for u in range(2)]
            s_hp = ev("s_hp")
            s_hid = ev("s_hid")
            s_y = ev("s_y")
            s_acc = ev("s_acc")
            s_out = [[ev(f"s_out{u}{j}") for j in range(4)] for u in range(2)]

            def list_plan(eng, t):
                return (eng.value_load(fplan[0:1, bass.ds(t, 1)], min_val=0, max_val=EF // FU + 1),
                        eng.value_load(fplan[0:1, bass.ds(t + NT, 1)], min_val=0, max_val=LIST_BLOCKS))

            def block_no(b):
                return nc.s_assert_within(b, 0, LIST_BLOCKS - 1, skip_runtime_bounds_check_because=
                                          "LIST_BLOCKS covers the blocks of any edges")

            @block.sync
            def _(sp):
                for to, of in ((b1_sb[:], b1), (b2_sb[:], b2), (bg[:], row_of(b_gat, 16)), (lg[:], row_of(ln_g, 16)),
                               (lb[:], row_of(ln_b, 16))):
                    sp.dma_start(to, of).then_inc(s_pl, 16)
                def group(g, u):
                    for j in range(4):
                        t = g * 4 + j
                        if j == 0:
                            sp.wait_ge(s_hp, g * 16)
                            for i in range(4):
                                sp.dma_start(x2g[u][:, :, i, :], x2_turned[bass.ds(t + i, 1), :, :]
                                             .rearrange("o p (k n) -> p (o k) n", k=2)).then_inc(s_x2l[u], 16)
                        sp.wait_ge(s_acc, t + 1)
                        sp.dma_start(x1g[u][:, j, :], x1_rows[bass.ds(t * NP, NP), :]).then_inc(s_x1l[u][j], 16)
                        sp.wait_ge(s_ownf, t + 1)
                        sp.dma_start(own[:, j, :], route_rows[bass.ds(t * NP, NP), :]).then_inc(s_own[j], 16)
                        blocks, before = list_plan(sp, t)
                        def one_block(b):
                            k = block_no(b + before)
                            sp.wait_ge(s_lused, k + 1)
                            sp.dma_start(lst[:, bass.ds(k % 16, 1), :].rearrange("p o c -> p (o c)"),
                                         lists[bass.ds(k * BLK, BLK), :].rearrange("(p c) o -> p (c o)", p=NP)).then_inc(s_ld, 16)
                            sp.wait_ge(s_ld, k * 16 + 16)
                            sp.sem_inc(s_lst, 1)
                        repeat(sp, blocks, one_block)
                def store(g, u):
                    for j in range(4):
                        t = g * 4 + j
                        sp.wait_ge(s_acc, t + 9)
                        sp.dma_start(out[bass.ds(t * NP, NP), :], acc[u][:, j, :]).then_inc(s_out[u][j], 16)

                steps(sp, NG, 2, [(2, store), (0, group)])
                for u in range(2):
                    for j in range(4):
                        sp.wait_ge(s_out[u][j], 16 * ((NG + 1 - u) // 2))
                for u in range(4):
                    sp.wait_ge(s_own[u], 16 * NG)

            @block.gpsimd
            def _(pool):
                nc.gpsimd.memset(first_e[:], 1.0).then_inc(s_fe, 1)
                pool.wait_ge(s_fe, 1)
                nc.gpsimd.affine_select(out=first_e[:], in_=first_e[:], compare_op=ALU.is_gt, fill=0.0, base=0,
                                        pattern=[[1, 4], [-1, 4]], channel_multiplier=0).then_inc(s_fe, 1)
                pool.sem_inc(s_lused, 16)
                with pool.Fori(0, NT) as t:
                    blocks, before = list_plan(pool, t)
                    def one_block(b):
                        k = block_no(b + before)
                        pool.wait_ge(s_lst, k + 1)
                        pool.sem_inc(s_gate, 1)
                        for h in range(2):
                            pool.wait_ge(s_half, k * 2 + (h + 1))
                            pool.sem_inc(s_gate, 1)
                            ins = nc.gpsimd.tensor_copy(ix[:, 3 * h:3 * h + 3],
                                                        lst[:, bass.ds(k % 16, 1), 3 * h:3 * h + 3].rearrange("p o c -> p (o c)"))
                            ins.then_inc(s_ixc, 1)
                            pool.wait_ge(s_ixc, k * 2 + (h + 1))
                            pool.sem_inc(s_gate, 1)
                            if h == 1:
                                pool.sem_inc(s_lused, 1)
                            for q in range(3):
                                pool.indirect_dma_start(out=nb_rows[h][:, q, :], out_offset=None, in_=route_rows,
                                                        in_offset=bass.IndirectOffsetOnAxis(ap=ix[:, 3 * h + q:3 * h + q + 1], axis=0)
                                                        ).then_inc(s_nb[3 * h + q], 16)

                    repeat(pool, blocks, one_block)
            @block.vector
            def _(dve):
                v = nc.vector
                dve.sem_inc(s_half, 2)
                dve.sem_inc(s_ownf, 4)
                dve.sem_inc(s_acc, 8)
                dve.wait_ge(s_pl, 5 * 16)
                dve.wait_ge(s_fe, 2)

                def attend(g, j):
                    t = g * 4 + j
                    dve.wait_ge(s_own[j], g * 16 + 16)
                    v.tensor_copy(nb_rows[0][:, 3, :], own[:, j, :]).then_inc(s_ownf, 1)
                    v.tensor_copy(ad[:], adst[:, bass.ds(t, 1), :].rearrange("p o h -> p (o h)"))
                    v.drain()
                    blocks, before = list_plan(dve, t)
                    def one_block(b):
                        k = block_no(b + before)
                        for h in range(2):
                            r, nxt = nb_rows[h], nb_rows[1 - h]
                            for q in range(3):
                                dve.wait_ge(s_nb[3 * h + q], k * 16 + 16)
                            v.tensor_reduce(r[:, 4, 20:24], r[:, 0:4, 20:24].rearrange("p r h -> p h r"), AX.X, ALU.max)
                            v.drain()
                            v.tensor_tensor(lk[:], r[:, :, 20:24], ad[:].rearrange("p (o h) -> p o h", o=1).broadcast_to([NP, 5, 4]), ALU.add)
                            v.tensor_copy(nxt[:, 3, 20:24], r[:, 4, 20:24])
                            v.drain()
                            v.scalar_tensor_tensor(out=lk[:], in0=lk[:], scalar=0.2, in1=lk[:], op0=ALU.mult, op1=ALU.max)
                            v.drain()
                            v.tensor_tensor(dif[:], lk[:, 0:4, :], lk[:, 4:5, :].broadcast_to([NP, 4, 4]), ALU.subtract).then_inc(s_dif, 1)
                            dve.wait_ge(s_pr, k * 2 + (h + 1))
                            v.tensor_tensor(msg[:].rearrange("p r (h e) -> p r h e", e=5),
                                            r[:, 0:4, 0:20].rearrange("p r (h e) -> p r h e", e=5),
                                            pr[:].rearrange("p r (h o) -> p r h o", o=1).broadcast_to([NP, 4, 4, 5]), ALU.mult)
                            v.drain()
                            v.tensor_reduce(nxt[:, 3, 0:20], msg[:].rearrange("p r c -> p c r"), AX.X, ALU.add)
                            v.drain()
                            dve.sem_inc(s_half, 1)
                    repeat(dve, blocks, one_block)
                    v.tensor_copy(res[:, j, :], nb_rows[0][:, 3, :])
                    v.drain()

                def weigh(g, u):
                    q5 = res[:, :, 0:20].rearrange("p t (h e) -> p t h e", e=5)
                    by_head = lambda a: a[:].rearrange("p t (h e) -> p t h e", e=4)
                    bc = lambda a: a[:].rearrange("p (o c) -> p o c", o=1).broadcast_to([NP, 4, 16])
                    v.tensor_scalar(rden[:].rearrange("p t (h o) -> p t h o", o=1), q5[:, :, :, 4:5], 1e-16, None, ALU.add)
                    v.drain()
                    v.reciprocal(rden[:], rden[:])
                    v.drain()
                    v.tensor_tensor(by_head(agg), q5[:, :, :, 0:4],
                                    rden[:].rearrange("p t (h o) -> p t h o", o=1).broadcast_to([NP, 4, 4, 4]), ALU.mult)
                    v.drain()
                    v.tensor_tensor(agg[:], agg[:], bc(bg), ALU.add)
                    v.drain()
                    v.tensor_reduce(m4[:], agg[:], AX.X, ALU.add)
                    v.drain()
                    v.tensor_scalar(m4[:], m4[:], 1.0 / 16, None, ALU.mult)
                    v.drain()
                    v.tensor_tensor(agg[:], agg[:], along(m4[:], 16), ALU.subtract)
                    v.drain()
                    v.tensor_tensor(asq[:], agg[:], agg[:], ALU.mult)
                    v.drain()
                    v.tensor_reduce(v4[:], asq[:], AX.X, ALU.add).then_inc(s_var, 1)
                    dve.wait_ge(s_rt, g + 1)
                    v.reciprocal(v4[:], v4[:])
                    v.drain()
                    v.tensor_tensor(agg[:], agg[:], along(v4[:], 16), ALU.mult)
                    v.drain()
                    v.tensor_tensor(agg[:], agg[:], bc(lg), ALU.mult)
                    v.drain()
                    v.tensor_tensor(agg[:], agg[:], bc(lb), ALU.add)
                    v.drain()
                    v.tensor_reduce(sc[:], agg[:].rearrange("p t (h e) -> p t e h", e=4), AX.X, ALU.add)
                    v.drain()
                    v.tensor_scalar(sc[:], sc[:], 0.25, None, ALU.mult)
                    v.drain()
                    other = sc[:].rearrange("p t (o j) -> p t o j", o=1).broadcast_to([NP, 4, 4, 4])
                    this = sc[:].rearrange("p t (e o) -> p t e o", o=1).broadcast_to([NP, 4, 4, 4])
                    v.tensor_tensor(gt[:], other, this, ALU.is_gt)
                    v.tensor_tensor(eq[:], other, this, ALU.is_equal)
                    v.tensor_reduce(m4[:], sc[:], AX.X, ALU.max)
                    v.drain()
                    for t in range(4):
                        v.tensor_tensor(eq[:, t, :, :], eq[:, t, :, :], first_e[:], ALU.mult)
                    v.tensor_tensor(sx[:], sc[:], along(m4[:], 4), ALU.subtract).then_inc(s_ex, 1)
                    v.drain()
                    v.tensor_tensor(gt[:], gt[:], eq[:], ALU.add)
                    v.drain()
                    v.tensor_reduce(rank[:], gt[:], AX.X, ALU.add)
                    v.drain()
                    dve.wait_ge(s_exd, g + 1)
                    v.scalar_tensor_tensor(out=sx[:], in0=rank[:], scalar=1.5, in1=sx[:], op0=ALU.is_lt, op1=ALU.mult)
                    v.drain()
                    v.tensor_reduce(m4[:], sx[:], AX.X, ALU.add)
                    v.drain()
                    v.reciprocal(m4[:], m4[:])
                    v.drain()
                    v.tensor_tensor(gate[u][:], sx[:], along(m4[:], 4), ALU.mult).then_inc(s_gate_r, 1)

                def combine(g, u, j):
                    Y = Y0 if j % 2 == 0 else Y1
                    dve.wait_ge(s_x1l[u][j], (g - u) * 8 + 16)
                    wait_after(dve, s_out[u][j], (g - u) * 8)
                    dve.wait_ge(s_y, g * 4 + (j + 1))
                    v.tensor_tensor(acc[u][:, j, :], x1g[u][:, j, :], B2[0:NP, 0:D], ALU.add)
                    for e in range(NE):
                        v.drain()
                        last = v.scalar_tensor_tensor(out=acc[u][:, j, :], in0=Y[e // 2][0:NP, (e % 2) * D:(e % 2 + 1) * D],
                                                      scalar=gate[u][:, j, e:e + 1], in1=acc[u][:, j, :], op0=ALU.mult, op1=ALU.add)
                    last.then_inc(s_acc, 1)

                steps(dve, NG, 2, [s for j in range(4) for s in (
                    (0, lambda g, u, j=j: attend(g, j)), (1, lambda g, u, j=j: combine(g, u, j)))] + [(0, weigh)])

            @block.scalar
            def _(act):
                a = nc.scalar.activation
                act.sem_inc(s_hid, 2)

                def gelus(g, u, e):
                    for c in range(4 * e, 4 * e + 4):
                        act.wait_ge(s_hp, g * 16 + (c + 17))
                        a(hid[u][:, c, :], HP[c % 2][:, 0:4 * NP], ACT.Gelu, bias=b1_sb[:, c:c + 1]).then_inc(s_hid, 1)

                def exps(g, j):
                    blocks, before = list_plan(act, g * 4 + j)
                    def one_block(b):
                        k = block_no(b + before)
                        for h in range(2):
                            act.wait_ge(s_dif, k * 2 + (h + 1))
                            a(pr[:], dif[:], ACT.Exp).then_inc(s_pr, 1)

                    repeat(act, blocks, one_block)
                def weigh(g, u):
                    act.wait_ge(s_var, g + 1)
                    a(v4[:], v4[:], ACT.Sqrt, bias=eps_c[0:NP, :], scale=1.0 / 16).then_inc(s_rt, 1)
                    act.wait_ge(s_ex, g + 1)
                    a(sx[:], sx[:], ACT.Exp).then_inc(s_exd, 1)

                def gate_copy(g, u):
                    act.wait_ge(s_gt, g + 1)
                    a(gate_t[u][:], GT[0:4, 0:4 * NP], ACT.Copy).then_inc(s_gtc, 1)

                act.wait_ge(s_pl, 5 * 16)
                steps(act, NG, 2, [(1, gate_copy)] + [s for j in range(4) for s in (
                    (0, lambda g, u, j=j: gelus(g, u, j)), (0, lambda g, u, j=j: exps(g, j)))] + [(0, weigh)])

            @block.tensor
            def _(pe):
                mm = nc.tensor.matmul
                pe.sem_inc(s_hp, 16)
                pe.wait_ge(s_pl, 5 * 16)

                def turn_gate(g, u):
                    pe.wait_ge(s_gate_r, g + 1)
                    for j in range(4):
                        last = nc.tensor.transpose(GT[0:4, j * NP:(j + 1) * NP], gate[u][:, j, :], ident[0:NP, 0:NP])
                    last.then_inc(s_gt, 1)

                def outputs(g, u, j):
                    Y = Y0 if j % 2 == 0 else Y1
                    if j == 0:
                        pe.wait_ge(s_gtc, g + 1)
                        pe.wait_ge(s_hid, g * 16 + 18)
                    pe.wait_ge(s_acc, g * 4 + (j + 7))
                    for e in range(NE):
                        for k in range(4):
                            mm(Y[e // 2][0:NP, (e % 2) * D:(e % 2 + 1) * D], hid[u][:, 4 * e + k, j * NP:(j + 1) * NP],
                               w2_sb[:, e, k, :], start=k == 0, stop=k == 3)
                    pe.wait_ge(s_acc, g * 4 + (j + 8))
                    mm(B2[0:NP, 0:D], gate_t[u][:, j * NP:(j + 1) * NP], b2_sb[:], start=True, stop=True).then_inc(s_y, 1)

                def hidden(g, u, e):
                    if e == 0:
                        pe.wait_ge(s_x2l[u], (g - u) * 32 + 64)
                    for c in range(4 * e, 4 * e + 4):
                        pe.wait_ge(s_hid, g * 16 + (c + 1))
                        for k in range(2):
                            last = mm(HP[c % 2][:, 0:4 * NP], w1_sb[:, k, e, (c % 4) * P:(c % 4 + 1) * P],
                                      x2g[u][:, k, :, :].rearrange("p j n -> p (j n)"), start=k == 0, stop=k == 1)
                        last.then_inc(s_hp, 1)

                steps(pe, NG, 2, [(1, turn_gate)] + [s for j in range(4) for s in (
                    (1, lambda g, u, j=j: outputs(g, u, j)), (0, lambda g, u, j=j: hidden(g, u, j)))])



_INS = ["x", "src", "dst", "L0_gnn_weight", "L0_gnn_bias", "L0_mix_Wqkv", "kv_turned", "out_turned", "L0_mix_bout",
        "L0_ffn_W_gat", "L0_ffn_att_src", "L0_ffn_att_dst", "L0_ffn_b_gat", "L0_ffn_ln_gamma", "L0_ffn_ln_beta",
        "L0_ffn_W1", "b1_cols", "L0_ffn_W2", "L0_ffn_b2", "L0_ffn_edge_index"]


def kernel(**inputs):
    import numpy as np
    import concourse.bacc as bacc
    from concourse.bass_utils import run_bass_kernel_spmd

    given = {k: np.asarray(v) for k, v in inputs.items()}
    given["kv_turned"] = given["L0_mix_Wqkv"][INNER:].T
    given["out_turned"] = given["L0_mix_Wout"].T
    given["b1_cols"] = given["L0_ffn_b1"].reshape(NE * 4, P).T
    nc = bacc.Bacc("TRN2", target_bir_lowering=False, num_devices=1)
    arrays, args = {}, []
    for name in _INS:
        a = np.ascontiguousarray(given[name])
        arrays[f"in_{name}"] = a
        args.append(nc.dram_tensor(f"in_{name}", a.shape, mybir.dt.from_np(a.dtype), kind="ExternalInput").ap())
    args.append(nc.dram_tensor("out", (N, D), f32, kind="ExternalOutput").ap())
    build(nc, *args)
    r = run_bass_kernel_spmd(nc, [arrays], core_ids=[0])
    return r.results[0]["out"]


def dump(nc, dbg, tensors):
    with nc.semaphore("s_dump") as s, nc.Block() as b:
        @b.sync
        def _(sp):
            for n, (name, t) in enumerate(tensors.items()):
                t = t[:] if "Handle" in type(t).__name__ else t
                shape = list(t.shape)
                o = nc.dram_tensor("dbg_" + name, shape, t.dtype, kind="ExternalOutput").ap()
                sp.dma_start(o, t).then_inc(s, 16)
                sp.wait_ge(s, 16 * n + 16)
                dbg["names"].append("dbg_" + name)
```

```python
import concourse.bass as bass
from concourse import mybir
from contextlib import ExitStack

f32 = mybir.dt.float32
i32 = mybir.dt.int32
bf16 = mybir.dt.bfloat16
ALU = mybir.AluOpType
ACT = mybir.ActivationFunctionType
AX = mybir.AxisListType

N, D = 12500, 256
NP = 125
NT = N // NP
NG = NT // 4
P = 128
EG = 212500
EF = 131072
GC = 1664
GJ = GC // P
FC = EF // P
FJ = FC // P
HEADS, DH = 8, 64
INNER = HEADS * DH
NE, FH = 4, 512
RH = 4
ROW = 24
FAR = 16000.0
NEG = -1.0e30
MAGIC = 12582912.0
EPS = 1e-5
GU = 9
FU = 7
RING = 8
PRE = FC // 8 - NT - 1
GW = GC + GU
LIST_BLOCKS = (EF // FU + NT + 2 * RING + P) // P * P
BLK = NP * FU


def steps(eng, n, unroll, stages):
    depth = max(lag for lag, _ in stages)
    head = -(-depth // unroll) * unroll
    body = (n - head) // unroll

    def step(s, slot, static):
        for lag, emit in stages:
            if static is None or 0 <= static - lag < n:
                emit(s - lag, (slot - lag) % unroll)

    for s in range(head):
        step(s, s % unroll, s)
    with eng.Fori(0, body) as i:
        for u in range(unroll):
            step(i * unroll + (head + u), u, None)
    for s in range(head + body * unroll, n + depth):
        step(s, s % unroll, s)


def wait_after(eng, sem, value):
    if not (isinstance(value, int) and value <= 0):
        eng.wait_ge(sem, value)


def repeat(eng, count, body):
    with eng.If(count > 0):
        with eng.Fori(0, count) as i:
            body(i)


def to_all(row):
    return row.broadcast_to([P, row.shape[1]])


def along(a, n):
    return a.rearrange("p (m o) -> p m o", o=1).broadcast_to([a.shape[0], a.shape[1], n])


def row_of(a, n):
    return a.rearrange("(o f) -> o f", o=1).broadcast_to([NP, n])


def build(nc, x, src, dst, gnn_w, gnn_b, wqkv, wkv_t, wout_t, bout, w_gat, att_src, att_dst,
          b_gat, ln_g, ln_b, w1, b1, w2, b2, fedge, out):
    ctx = ExitStack()
    with ctx:
        sb = lambda name, shape, dt=f32: ctx.enter_context(nc.sbuf_tensor(name, shape, dt))
        pb = lambda name, shape, dt=f32: ctx.enter_context(nc.psum_tensor(name, shape, dt))
        sem = lambda name: ctx.enter_context(nc.semaphore(name))
        dram = lambda name, shape, dt=f32: nc.dram_tensor(name, shape, dt, kind="Internal").ap()

        xn_rows = dram("xn_rows", [N, D])
        x1_rows = dram("x1_rows", [N, D])
        route_rows = dram("route_rows", [N + 1, ROW])
        lists = dram("lists", [LIST_BLOCKS * BLK, 1], i32)
        xn_turned = dram("xn_turned", [NT, P, 2 * NP])
        x2_turned = dram("x2_turned", [NT, P, 2 * NP])
        hi_rows = dram("hi_rows", [FC, P], bf16)
        chunk_lo = dram("chunk_lo", [GC, 1])
        chunk_hi = dram("chunk_hi", [GC, 1])

        ident = sb("ident", [P, P])
        below = sb("below", [P, P])
        above = sb("above", [P, P])
        sooner = sb("sooner", [P, NT])
        turn = sb("turn", [P, NT])
        iota_j = sb("iota_j", [P, P])
        iota_p = sb("iota_p", [P, 1])
        neg_first = sb("neg_first", [P, NT])
        zeros_b = sb("zeros_b", [P, 512], bf16)
        eps_c = sb("eps_c", [P, 1])

        arena = sb("arena", [P, 8192])
        hi_e, lo_e, src_e, dst_e = (arena[:, k * FC:(k + 1) * FC] for k in range(4))
        wkv = arena[:, 4096:6144].rearrange("p (k f) -> p k f", k=2)
        wq = arena[:, 6144:7168].rearrange("p (k f) -> p k f", k=4)
        wo = arena[:, 7168:8192].rearrange("p (k f) -> p k f", k=4)
        w1_sb = arena[:, 0:4096].rearrange("p (k e f) -> p k e f", k=2, e=NE)
        w2_sb = arena[:, 4096:8192].rearrange("p (e k f) -> p e k f", e=NE, k=4)
        wg = sb("wg", [P, 4, D])
        mix = sb("mix", [P, 2, D])
        wr = sb("wr", [P, 2, ROW])
        att = sb("att", [P, 2, 16])
        bias_x = sb("bias_x", [P, D])
        bout_b = sb("bout_b", [P, D])
        gsrc = sb("gsrc", [P, GW], i32)
        gdst = sb("gdst", [P, GW])
        adst = sb("adst", [NP, NT, RH])
        gplan = sb("gplan", [1, 3 * NT], i32)
        fplan = sb("fplan", [1, 2 * NT + 1], i32)

        s_const = sem("s_const")
        s_w = sem("s_w")
        s_v = sem("s_v")
        s_gate = sem("s_gate")
        PS = [pb(f"PS{k}", [P, 512]) for k in range(8)]

        small = sb("small", [P, 64])
        pad_list = sb("pad_list", [P, BLK], i32)
        base8 = sb("base8", [P, 1])

        oh_hi = sb("oh_hi", [P, 8, NT], bf16)
        oh_lo = sb("oh_lo", [P, 8, NP], bf16)
        dst_b = [sb(f"dst_b{h}", [P, 512], i32) for h in range(2)]
        hi_bc = [sb(f"hi_bc{h}", [P, 512], bf16) for h in range(2)]
        oh_t = [sb(f"oh_t{h}", [NT, 512]) for h in range(2)]
        t_sb = [sb(f"t_sb{k}", [NT, NP]) for k in range(2)]
        rk = sb("rk", [P, 8])
        tv = sb("tv", [P, 8])
        junk = sb("junk", [P, 8, P], bf16)
        junk_l = sb("junk_l", [P, 8, P], bf16)
        pos_f = sb("pos_f", [P, 8])
        blk_f = sb("blk_f", [P, 8])
        pos_i = sb("pos_i", [P, 8], i32)
        val_i = sb("val_i", [P, 8], i32)

        setup = ExitStack()
        flat = setup.enter_context(nc.sbuf_tensor("flat", [P, 2 * N], f32))[:]
        at = [0]

        def take(cols, dt=f32):
            v = flat[:, at[0]:at[0] + cols]
            at[0] += cols
            assert at[0] <= 2 * N
            return v if dt == f32 else v.bitcast(dt)

        tiles = lambda v: v.rearrange("p (j e) -> p j e", e=P)
        gd_i, gs_i = tiles(take(GC, i32)), tiles(take(GC, i32))
        g_f, gs_f = tiles(take(GC)), tiles(take(GC))
        fd_i, fs_i = tiles(take(FC, i32)), tiles(take(FC, i32))
        f_d, f_s, f_hi, f_lo = (tiles(take(FC)) for _ in range(4))
        f_hib = tiles(take(FC // 2, bf16))
        gh, gt = tiles(take(GC)), tiles(take(GC))
        lo_b, hi_b = flat[:, 0:GC], flat[:, GC:2 * GC]
        m_b, chunk_no, cand = take(GC), take(GC), take(GC)

        CNT, SM = PS[2], PS[3]

        turned = []
        for of, to, n in ((f_hi, hi_e, FJ), (f_lo, lo_e, FJ), (f_s, src_e, FJ), (f_d, dst_e, FJ),
                          (g_f, gdst, GJ), (gs_f, gsrc, GJ)):
            for k in range(0, n, 4):
                m = min(4, n - k)
                turned.append((of[:, k:k + m, :], to[:, k * P:(k + m) * P], m))
        n_router = 4 * FJ // 4

        s_fd = sem("s_fd")
        s_gd = sem("s_gd")
        s_ff = sem("s_ff")
        s_gf = sem("s_gf")
        s_tr = sem("s_tr")
        s_trc = sem("s_trc")
        s_hist = sem("s_hist")
        s_histm = sem("s_histm")
        s_base = sem("s_base")
        s_basev = sem("s_basev")
        s_cr = sem("s_cr")
        s_crb = sem("s_crb")
        s_gp = sem("s_gp")
        s_gpm = sem("s_gpm")
        s_hirow = sem("s_hirow")
        s_pad = sem("s_pad")

        with nc.Block() as block:
            @block.sync
            def _(sp):
                FULL = EG // (P * P) * P * P
                left = EG - FULL
                rows = left // P
                sp.wait_ge(s_v, 1)
                for t_i, a in ((gd_i, dst), (gs_i, src)):
                    sp.dma_start(t_i[:, 0:GJ - 1, :], a[0:FULL].rearrange("(j p e) -> p j e", p=P, e=P)).then_inc(s_gd, 16)
                    sp.dma_start(t_i[0:rows, GJ - 1, :], a[FULL:FULL + rows * P].rearrange("(p e) -> p e", e=P)).then_inc(s_gd, 16)
                    sp.dma_start(t_i[rows:rows + 1, GJ - 1, 0:left - rows * P],
                                 a[FULL + rows * P:EG].rearrange("(p e) -> p e", p=1)).then_inc(s_gd, 16)
                for t_i, k in ((fd_i, 1), (fs_i, 0)):
                    sp.dma_start(t_i, fedge[k, :].rearrange("(j p e) -> p j e", p=P, e=P)).then_inc(s_fd, 16)
                sp.dma_start(wkv, wkv_t.rearrange("(k p) f -> p k f", p=P)).then_inc(s_w, 16)
                sp.dma_start(wq, wqkv[0:INNER, :].rearrange("(k p) f -> p k f", p=P)).then_inc(s_w, 16)
                sp.dma_start(wo, wout_t.rearrange("(k p) f -> p k f", p=P)).then_inc(s_w, 16)
                sp.dma_start(wg[:], gnn_w.rearrange("(k p) f -> p k f", p=P)).then_inc(s_w, 16)
                sp.dma_start(wr[:, :, 0:16], w_gat.rearrange("(k p) f -> p k f", p=P)).then_inc(s_w, 16)
                sp.dma_start(att[:, 0, :], to_all(att_src.rearrange("(o h) e -> o (h e)", o=1))).then_inc(s_w, 16)
                sp.dma_start(att[:, 1, :], to_all(att_dst.rearrange("(o h) e -> o (h e)", o=1))).then_inc(s_w, 16)
                sp.dma_start(bias_x[:], to_all(gnn_b.rearrange("(o f) -> o f", o=1))).then_inc(s_w, 16)
                sp.dma_start(bout_b[:], to_all(bout.rearrange("(o f) -> o f", o=1))).then_inc(s_w, 16)
                sp.wait_ge(s_ff, 1)
                sp.dma_start(hi_rows.rearrange("(j p) e -> p j e", p=P), f_hib).then_inc(s_hirow, 16)
                sp.wait_ge(s_gf, 1)
                sp.dma_start(chunk_lo.rearrange("(p j) o -> p (j o)", p=P), small[:, 0:GJ]).then_inc(s_cr, 16)
                sp.dma_start(chunk_hi.rearrange("(p j) o -> p (j o)", p=P), small[:, 16:16 + GJ]).then_inc(s_cr, 16)
                sp.wait_ge(s_cr, 32)
                sp.dma_start(lo_b, to_all(chunk_lo.rearrange("c o -> o c"))).then_inc(s_crb, 16)
                sp.dma_start(hi_b, to_all(chunk_hi.rearrange("c o -> o c"))).then_inc(s_crb, 16)
                sp.wait_ge(s_hirow, 16)

            @block.gpsimd
            def _(pool):
                nc.gpsimd.memset(ident[:], 0.0)
                nc.gpsimd.memset(below[:], 1.0)
                nc.gpsimd.memset(above[:], 1.0)
                nc.gpsimd.iota(iota_j[:], [[1, P]], base=0, channel_multiplier=0, allow_small_or_imprecise_dtypes=True)
                nc.gpsimd.iota(turn[:], [[1, 4], [4, NG]], base=0, channel_multiplier=0, allow_small_or_imprecise_dtypes=True)
                nc.gpsimd.iota(iota_p[:], [[0, 1]], base=0, channel_multiplier=1, allow_small_or_imprecise_dtypes=True)
                nc.gpsimd.iota(neg_first[:], [[-NP, NT]], base=0, channel_multiplier=0, allow_small_or_imprecise_dtypes=True)
                nc.gpsimd.iota(pad_list[:], [[0, BLK]], base=N, channel_multiplier=0).then_inc(s_const, 1)
                pool.wait_ge(s_const, 1)
                nc.gpsimd.affine_select(out=ident[:], in_=ident[:], compare_op=ALU.not_equal, fill=1.0, base=0,
                                        pattern=[[-1, P]], channel_multiplier=1)
                nc.gpsimd.affine_select(out=below[:], in_=below[:], compare_op=ALU.is_gt, fill=0.0, base=0,
                                        pattern=[[-1, P]], channel_multiplier=1)
                nc.gpsimd.affine_select(out=above[:], in_=above[:], compare_op=ALU.is_gt, fill=0.0, base=0,
                                        pattern=[[1, P]], channel_multiplier=-1).then_inc(s_const, 1)

            @block.vector
            def _(dve):
                v = nc.vector
                v.memset(gd_i[:, GJ - 1, :], 16000)
                v.memset(gs_i[:, GJ - 1, :], 0).then_inc(s_v, 1)
                v.memset(zeros_b[:], 0.0)
                v.memset(eps_c[:], EPS).then_inc(s_v, 1)

                def tile_of(dst_f, hi, tmp):
                    v.tensor_scalar(tmp, dst_f, 1.0 / NP, 0.5 / NP - 0.5, ALU.mult, ALU.add)
                    v.drain()
                    v.tensor_scalar(hi, tmp, MAGIC, MAGIC, ALU.add, ALU.subtract)
                    v.drain()

                dve.wait_ge(s_fd, 32)
                v.tensor_copy(f_d, fd_i)
                v.tensor_copy(f_s, fs_i)
                v.drain()
                tile_of(f_d, f_hi, f_lo)
                v.tensor_copy(f_hib, f_hi)
                v.scalar_tensor_tensor(out=f_lo, in0=f_hi, scalar=-float(NP), in1=f_d, op0=ALU.mult, op1=ALU.add)
                v.drain()
                v.memset(small[:, 60:61], 0.0).then_inc(s_ff, 1)
                def copy_out(first, last):
                    for k in range(first, last):
                        _, to, n = turned[k]
                        dve.wait_ge(s_tr, k + 1)
                        v.tensor_copy(to, PS[k % 2][:, 0:n * P]).then_inc(s_trc, 1)

                copy_out(0, n_router)
                dve.wait_ge(s_gd, 96)
                v.tensor_copy(g_f, gd_i)
                v.tensor_copy(gs_f, gs_i)
                v.drain()
                tile_of(g_f, gh, gt)
                v.tensor_reduce(small[:, 0:GJ], gh, AX.X, ALU.min)
                v.tensor_reduce(small[:, 16:16 + GJ], gh, AX.X, ALU.max)
                v.drain()
                v.memset(small[:, 61:62], 0.0).then_inc(s_gf, 1)
                copy_out(n_router, len(turned))
                dve.wait_ge(s_crb, 32)
                dve.wait_ge(s_gp, 1)
                v.tensor_scalar(m_b, lo_b, iota_p[:], None, ALU.is_le)
                v.drain()
                v.scalar_tensor_tensor(out=cand, in0=hi_b, scalar=iota_p[:], in1=m_b, op0=ALU.is_ge, op1=ALU.mult)
                v.drain()
                v.scalar_tensor_tensor(out=m_b, in0=chunk_no, scalar=-4096.0, in1=cand, op0=ALU.add, op1=ALU.mult)
                v.scalar_tensor_tensor(out=lo_b, in0=chunk_no, scalar=1.0, in1=cand, op0=ALU.add, op1=ALU.mult)
                v.drain()
                v.tensor_reduce(small[:, 40:41], m_b, AX.X, ALU.min)
                v.tensor_reduce(small[:, 41:42], lo_b, AX.X, ALU.max)
                v.drain()
                v.tensor_scalar(small[:, 42:43], small[:, 40:41], 4096.0, None, ALU.add)
                v.drain()
                v.tensor_tensor(small[:, 43:44], small[:, 41:42], small[:, 42:43], ALU.subtract)
                v.tensor_scalar(small[:, 44:45], small[:, 42:43], float(GC), None, ALU.min)
                v.drain()
                v.tensor_scalar(small[:, 45:46], small[:, 43:44], 0.0, None, ALU.max)
                v.drain()
                v.tensor_scalar(small[:, 46:47], small[:, 45:46], 1.0 / GU, (GU - 1) / (2.0 * GU), ALU.mult, ALU.add)
                v.drain()
                v.tensor_scalar(small[:, 45:46], small[:, 46:47], MAGIC, MAGIC, ALU.add, ALU.subtract)
                v.drain()
                v.memset(small[:, 63:64], 0.0).then_inc(s_gpm, 1)
                dve.wait_ge(s_gp, 2)
                v.tensor_copy(gplan[:, :], SM[0:1, 0:3 * NT])
                v.memset(gdst[:, GC:GW], FAR)
                v.memset(gsrc[:, GC:GW], 0)
                dve.wait_ge(s_w, 9 * 16)
                heads = wkv.rearrange("p k (h e) -> p (k h) e", e=DH)
                v.tensor_reduce(small[:, 0:32], heads, AX.X, ALU.add)
                v.drain()
                v.tensor_scalar(small[:, 0:32], small[:, 0:32], 1.0 / DH, None, ALU.mult)
                v.drain()
                v.tensor_tensor(heads, heads, along(small[:, 0:32], DH), ALU.subtract)
                v.tensor_tensor(bias_x[:], bias_x[:], bout_b[:], ALU.add)
                v.drain()
                for k in range(2):
                    for side in range(2):
                        v.tensor_tensor(small[:, 0:16], wr[:, k, 0:16], att[:, side, :], ALU.mult)
                        v.drain()
                        v.tensor_reduce(wr[:, k, 16 + 4 * side:20 + 4 * side],
                                        small[:, 0:16].rearrange("p (h e) -> p h e", e=4), AX.X, ALU.add)
                        v.drain()

            @block.tensor
            def _(pe):
                pe.wait_ge(s_const, 2)
                pe.wait_ge(s_ff, 1)
                for k, (of, _, n) in enumerate(turned):
                    if k == n_router:
                        pe.wait_ge(s_gf, 1)
                    if k >= 2:
                        pe.wait_ge(s_trc, k - 1)
                    for q in range(n):
                        last = nc.tensor.transpose(PS[k % 2][:, q * P:(q + 1) * P], of[:, q, :], ident[:])
                    last.then_inc(s_tr, 1)
                pe.wait_ge(s_gpm, 1)
                c0, ng = small[0:NT, 44:45], small[0:NT, 45:46]
                nc.tensor.matmul(SM[0:1, 0:NT], c0, ident[0:NT, 0:NT], start=True, stop=True)
                nc.tensor.matmul(SM[0:1, NT:2 * NT], ng, ident[0:NT, 0:NT], start=True, stop=True)
                nc.tensor.matmul(SM[0:1, 2 * NT:3 * NT], ng, above[0:NT, 0:NT], start=True, stop=True).then_inc(s_gp, 1)

            @block.scalar
            def _(act):
                act.wait_ge(s_const, 2)
                for j in range(GJ):
                    nc.scalar.activation(chunk_no.rearrange("q (p j) -> q j p", j=GJ)[:, j, :], iota_j[:], ACT.Copy, bias=float(j * P))
                act.drain()
                act.sem_inc(s_gp, 1)
        setup.close()

        with ExitStack() as stage, nc.Block() as block:
            two = lambda name, shape, dt=f32: [stage.enter_context(nc.sbuf_tensor(f"{name}{u}", shape, dt)) for u in range(2)]
            ev = lambda name: stage.enter_context(nc.semaphore(name))
            x_in, x_n = two("x_in", [NP, D]), two("x_n", [NP, D])
            st6, mv, rstd = two("st6", [NP, 6]), two("mv", [NP, 2]), two("rstd", [NP, 1])
            k_sb, v_sb, sq = two("k_sb", [NP, INNER]), two("v_sb", [NP, INNER]), two("sq", [NP, 2, INNER])
            ss, rr = two("ss", [NP, 16]), two("rr", [NP, 8])
            fold = two("fold", [NP, 16, DH // 2])
            x_t = two("x_t", [P, 2 * NP])
            s_fold = ev("s_fold")
            XT, KP, VP, DT = PS[0:2], PS[4:6], PS[6:8], PS[3]
            s_xl = [ev(f"s_xl{u}") for u in range(2)]
            s_xs = [ev(f"s_xs{u}") for u in range(2)]
            s_ts = [ev(f"s_ts{u}") for u in range(2)]
            s_var = ev("s_var")
            s_std = ev("s_std")
            s_xn = ev("s_xn")
            s_turn = ev("s_turn")
            s_turnc = ev("s_turnc")
            s_kv = ev("s_kv")
            s_sq = ev("s_sq")
            s_ss = ev("s_ss")
            s_kc = ev("s_kc")
            s_rt = ev("s_rt")
            s_vn = ev("s_vn")
            s_dt = ev("s_dt")
            s_oh = ev("s_oh")
            s_ohm = ev("s_ohm")

            @block.sync
            def _(sp):
                def load(t, u):
                    sp.wait_ge(s_xn, t + 1)
                    sp.dma_start(x_in[u][:], x[bass.ds(t * NP, NP), :]).then_inc(s_xl[u], 16)

                def store(t, u):
                    sp.wait_ge(s_xn, t + 3)
                    sp.dma_start(xn_rows[bass.ds(t * NP, NP), :], x_n[u][:]).then_inc(s_xs[u], 16)

                def store_turned(t, u):
                    sp.wait_ge(s_turnc, t + 3)
                    sp.dma_start(xn_turned[bass.ds(t, 1), :, :].rearrange("o p c -> p (o c)"), x_t[u][:]).then_inc(s_ts[u], 16)

                steps(sp, NT, 2, [(0, load), (1, store), (2, store_turned)])
                for u in range(2):
                    sp.wait_ge(s_ts[u], 16 * NT // 2)
                    sp.wait_ge(s_xs[u], 16 * NT // 2)

            @block.gpsimd
            def _(pool):
                def pairs(t, u):
                    pool.wait_ge(s_sq, t + 1)
                    pool.wait_ge(s_ss, t + 1)
                    heads = sq[u][:].rearrange("p s (h e) -> p (s h) e", e=DH)
                    nc.gpsimd.tensor_tensor(fold[u][:], heads[:, :, 0:DH // 2], heads[:, :, DH // 2:DH], ALU.add).then_inc(s_fold, 1)

                steps(pool, NT, 2, [(0, pairs)])

            def hist(dve, i, halves=(0, 1)):
                v = nc.vector
                for h in halves:
                    dve.wait_ge(s_ohm, i * 2 + (h + 1))
                    for to, of, n in ((oh_hi, hi_e, NT), (oh_lo, lo_e, NP)):
                        last = v.tensor_tensor(to[:, 4 * h:4 * h + 4, :],
                                               iota_j[:, 0:n].rearrange("p (o n) -> p o n", o=1).broadcast_to([P, 4, n]),
                                               along(of[:, bass.ds(i * 8 + 4 * h, 4)], n), ALU.is_equal)
                    last.then_inc(s_oh, 1)

            @block.vector
            def _(dve):
                v = nc.vector
                dve.sem_inc(s_xn, 2)
                dve.sem_inc(s_vn, 2)
                dve.sem_inc(s_ss, 2)

                def stats(t, u):
                    dve.wait_ge(s_xl[u], (t - u) * 8 + 16)
                    v.bn_stats(st6[u][:], x_in[u][:])
                    v.drain()
                    v.bn_aggr(mv[u][:], st6[u][:]).then_inc(s_var, 1)

                def norm(t, u):
                    dve.wait_ge(s_std, t + 1)
                    v.reciprocal(rstd[u][:], rstd[u][:])
                    v.drain()
                    wait_after(dve, s_xs[u], (t - u) * 8)
                    v.tensor_scalar(x_n[u][:], x_in[u][:], mv[u][:, 0:1], rstd[u][:], ALU.subtract, ALU.mult).then_inc(s_xn, 1)

                def spread(t, u):
                    dve.wait_ge(s_fold, t + 1)
                    v.tensor_reduce(ss[u][:], fold[u][:], AX.X, ALU.add).then_inc(s_ss, 1)

                def values(t, u):
                    dve.wait_ge(s_rt, t + 1)
                    v.reciprocal(ss[u][:], ss[u][:])
                    v.drain()
                    v.tensor_tensor(rr[u][:], ss[u][:, 0:8], ss[u][:, 8:16], ALU.mult)
                    v.drain()
                    dve.wait_ge(s_dt, t + 1)
                    v.tensor_tensor(v_sb[u][:].rearrange("p (h e) -> p h e", e=DH),
                                    VP[u][0:NP, :].rearrange("p (h e) -> p h e", e=DH), along(rr[u][:], DH),
                                    ALU.mult).then_inc(s_vn, 1)

                steps(dve, NT, 2, [(0, stats), (0, lambda t, u: hist(dve, t, (0,))), (0, norm), (3, spread),
                                   (0, lambda t, u: hist(dve, t, (1,))), (3, values)])
                with dve.Fori(NT, FC // 8) as i:
                    hist(dve, i)

            @block.scalar
            def _(act):
                a = nc.scalar.activation
                act.sem_inc(s_turnc, 2)

                def std(t, u):
                    act.wait_ge(s_var, t + 1)
                    a(rstd[u][:], mv[u][:, 1:2], ACT.Sqrt, bias=eps_c[0:NP, :]).then_inc(s_std, 1)

                def turn_copy(t, u):
                    act.wait_ge(s_turn, t + 1)
                    wait_after(act, s_ts[u], (t - u) * 8)
                    a(x_t[u][:], XT[u][:, 0:2 * NP], ACT.Copy).then_inc(s_turnc, 1)

                def squares(t, u):
                    act.wait_ge(s_kv, t + 1)
                    wait_after(act, s_fold, t - 1)
                    a(sq[u][:, 0, :], KP[u][0:NP, :], ACT.Square)
                    a(sq[u][:, 1, :], VP[u][0:NP, :], ACT.Square).then_inc(s_sq, 1)
                    act.wait_ge(s_dt, t + 1)
                    a(k_sb[u][:], KP[u][0:NP, :], ACT.Copy).then_inc(s_kc, 1)

                def roots(t, u):
                    act.wait_ge(s_ss, t + 3)
                    a(ss[u][:], ss[u][:], ACT.Sqrt, bias=eps_c[0:NP, :], scale=1.0 / DH).then_inc(s_rt, 1)

                steps(act, NT, 2, [(0, std), (1, turn_copy), (3, roots), (2, squares)])

            def count(pe, i):
                for h in range(2):
                    pe.wait_ge(s_oh, i * 2 + (h + 1))
                    for q in range(4 * h, 4 * h + 4):
                        last = nc.tensor.matmul(CNT[0:NT, 0:NP], oh_hi[:, q, :], oh_lo[:, q, :], start=False, stop=False)
                    last.then_inc(s_ohm, 1)

            @block.tensor
            def _(pe):
                mm = nc.tensor.matmul
                zero = lambda to, m, n, **kw: mm(to, zeros_b[:, 0:m], zeros_b[:, 0:n], **kw)
                zero(CNT[0:NT, 0:NP], NT, NP, start=True, stop=False)
                zero(DT[:, :], P, 512, start=True, stop=False)
                pe.sem_inc(s_ohm, 2)
                pe.sem_inc(s_dt, 2)

                def turn(t, u):
                    pe.wait_ge(s_xn, t + 3)
                    pe.wait_ge(s_turnc, t + 1)
                    for k in range(2):
                        last = nc.tensor.transpose(XT[u][:, k * NP:(k + 1) * NP], x_n[u][:, k * P:(k + 1) * P],
                                                   ident[0:NP, 0:NP])
                    last.then_inc(s_turn, 1)

                def keys_values(t, u):
                    pe.wait_ge(s_turnc, t + 3)
                    pe.wait_ge(s_vn, t + 1)
                    for k in range(2):
                        mm(KP[u][0:NP, :], x_t[u][:, k * NP:(k + 1) * NP], wkv[:, k, 0:INNER], start=k == 0, stop=k == 1)
                    for k in range(2):
                        last = mm(VP[u][0:NP, :], x_t[u][:, k * NP:(k + 1) * NP], wkv[:, k, INNER:2 * INNER],
                                  start=k == 0, stop=k == 1)
                    last.then_inc(s_kv, 1)

                def outer(t, u):
                    pe.wait_ge(s_kc, t + 1)
                    pe.wait_ge(s_vn, t + 3)
                    for q in range(4):
                        last = mm(DT[:, q * P:(q + 1) * P], v_sb[u][:, q * P:(q + 1) * P], k_sb[u][:, q * P:(q + 1) * P],
                                  start=False, stop=False)
                    last.then_inc(s_dt, 1)

                steps(pe, NT, 2, [(1, turn), (4, outer), (2, keys_values), (0, lambda t, u: count(pe, t))])
                with pe.Fori(NT, FC // 8) as i:
                    count(pe, i)
                zero(CNT[0:NT, 0:NP], NT, NP, start=False, stop=True)
                zero(DT[:, :], P, 512, start=False, stop=True)

        with ExitStack() as stage, nc.Block() as block:
            ev = lambda name: stage.enter_context(nc.semaphore(name))
            dt_sb = stage.enter_context(nc.sbuf_tensor("dt_sb", [P, 4, P], f32))
            u_sb = stage.enter_context(nc.sbuf_tensor("u_sb", [P, 4, D], f32))
            UP, MP = PS[4:6], PS[6]
            s_nb = ev("s_nb")
            s_plan = ev("s_plan")
            s_plan_sb = ev("s_plan_sb")
            s_fill = ev("s_fill")
            s_dts = ev("s_dts")
            s_u = ev("s_u")
            s_uc = ev("s_uc")
            s_m = ev("s_m")
            s_t0 = ev("s_t0")

            @block.sync
            def _(sp):
                sp.wait_ge(s_plan_sb, 1)
                rounds = sp.value_load(fplan[0:1, 2 * NT:2 * NT + 1], min_val=0, max_val=LIST_BLOCKS // P)
                def one_round(b):
                    sp.dma_start(lists[bass.ds(b * (P * BLK), P * BLK), :].rearrange("(p e) o -> p (e o)", p=P),
                                 pad_list[:]).then_inc(s_fill, 16)
                    sp.wait_ge(s_fill, b * 16 + 16)
                    sp.sem_inc(s_gate, 1)
                repeat(sp, rounds, one_round)

            @block.vector
            def _(dve):
                v = nc.vector
                v.tensor_tensor(sooner[:], turn[:], ident[:, 0:NT], ALU.mult)
                v.drain()
                v.tensor_reduce(small[:, 38:39], sooner[:], AX.X, ALU.add)
                v.drain()
                v.tensor_scalar(sooner[:], turn[:], small[:, 38:39], None, ALU.is_gt)
                v.tensor_reduce(small[0:NT, 32:33], CNT[0:NT, 0:NP], AX.X, ALU.max)
                v.drain()
                v.tensor_scalar(small[0:NT, 33:34], small[0:NT, 32:33], 1.0 / FU, (FU - 1) / (2.0 * FU), ALU.mult, ALU.add)
                v.drain()
                v.tensor_scalar(small[0:NT, 34:35], small[0:NT, 33:34], MAGIC, MAGIC, ALU.add, ALU.subtract).then_inc(s_nb, 1)
                dve.wait_ge(s_plan, 1)
                v.tensor_scalar(base8[0:NT, :], UP[0][0:NT, 256:257], float(FU), None, ALU.mult)
                v.tensor_copy(fplan[0:1, 0:2 * NT], UP[0][0:1, 0:2 * NT])
                v.tensor_scalar(small[0:1, 36:37], UP[0][0:1, 260:261], 1.0 / P, (P - 1) / (2.0 * P) + 2.0 * RING / P, ALU.mult, ALU.add)
                v.drain()
                v.tensor_scalar(small[0:1, 37:38], small[0:1, 36:37], MAGIC, MAGIC, ALU.add, ALU.subtract)
                v.drain()
                v.tensor_copy(fplan[0:1, 2 * NT:2 * NT + 1], small[0:1, 37:38]).then_inc(s_plan_sb, 1)
                v.memset(dt_sb[:], 0.0)
                v.drain()
                for lo in (0, DH):
                    last = v.tensor_scalar(dt_sb[lo:lo + DH, :, lo:lo + DH],
                                           PS[3][lo:lo + DH, :].rearrange("p (q d) -> p q d", q=4)[:, :, lo:lo + DH],
                                           1.0 / N, None, ALU.mult)
                last.then_inc(s_dts, 1)
                for q in range(2):
                    dve.wait_ge(s_u, q + 1)
                    v.tensor_copy(u_sb[:, 2 * q:2 * q + 2, :], UP[q][:, :].rearrange("p (q f) -> p q f", q=2)).then_inc(s_uc, 1)
                dve.wait_ge(s_m, 1)
                v.tensor_copy(mix[:], MP[:, :].rearrange("p (k f) -> p k f", k=2))


            @block.scalar
            def _(act):
                a = nc.scalar.activation
                act.wait_ge(s_plan_sb, 1)
                a(t_sb[0][:], CNT[0:NT, 0:NP], ACT.Identity, bias=base8[0:NT, :], scale=0.0).then_inc(s_t0, 1)

            @block.tensor
            def _(pe):
                mm = nc.tensor.matmul
                pe.wait_ge(s_nb, 1)
                nb = small[0:NT, 34:35]
                mm(UP[0][0:1, 0:NT], nb, ident[0:NT, 0:NT], start=True, stop=True)
                mm(UP[0][0:1, NT:2 * NT], nb, sooner[0:NT, :], start=True, stop=True)
                mm(UP[0][0:1, 260:261], nb, above[0:NT, NT:NT + 1], start=True, stop=True)
                mm(UP[0][0:NT, 256:257], sooner[0:NT, :], nb, start=True, stop=True).then_inc(s_plan, 1)
                pe.wait_ge(s_dts, 1)
                for q in range(4):
                    last = mm(UP[q // 2][:, (q % 2) * D:(q % 2 + 1) * D], dt_sb[:, q, :], wo[:, q, :], start=True, stop=True)
                    if q % 2:
                        last.then_inc(s_u, 1)
                pe.wait_ge(s_uc, 2)
                for k in range(2):
                    for q in range(4):
                        last = mm(MP[:, k * D:(k + 1) * D], wq[:, q, k * P:(k + 1) * P], u_sb[:, q, :], start=q == 0, stop=q == 3)
                last.then_inc(s_m, 1)

                pe.wait_ge(s_t0, 1)
                mm(CNT[0:NT, 0:NP], zeros_b[:, 0:NT], zeros_b[:, 0:NP], start=True, stop=True)

        with ExitStack() as stage, nc.Block() as block:
            one = lambda name, shape, dt=f32: stage.enter_context(nc.sbuf_tensor(name, shape, dt))
            two = lambda name, shape, dt=f32: [one(f"{name}{u}", shape, dt) for u in range(2)]
            ev = lambda name: stage.enter_context(nc.semaphore(name))
            rows = one("rows", [P, GU, D + 1])
            oh = one("oh", [P, GU, NP])
            idx = one("idx", [P, GU], i32)
            s_sb, s_t, x_t, x_in = two("s_sb", [NP, D]), two("s_t", [P, 2 * NP]), two("x_tc", [P, 2 * NP]), two("x_inc", [NP, D])
            rdeg, ssq, rstd = two("rdeg", [NP, 1]), two("ssq", [NP, 1]), two("rstdc", [NP, 1])
            sq = two("sqc", [NP, D])
            x1, x2, x2_t = two("x1", [NP, D]), two("x2", [NP, D]), two("x2_t", [P, 2 * NP])
            st6, mv, rt = two("st6c", [NP, 6]), two("mvc", [NP, 2]), two("rt", [NP, ROW])
            pad_row = one("pad_row", [1, ROW])
            SUM, LOOK, H = PS[0:2], PS[5:7], PS[7]
            ST, X2 = PS[3][:, 0:2 * NP], PS[3][:, 256:256 + 2 * NP]
            G, MX = PS[4][0:NP, 0:D], PS[4][0:NP, D:2 * D]
            s_bl = [ev(f"s_bl{h}") for h in range(2)]
            s_blf = ev("s_blf")
            s_oht = ev("s_oht")
            s_oh = ev("s_oh2")
            s_tab = ev("s_tab")
            s_look = ev("s_look")
            s_cnt = ev("s_cnt")
            s_sel = ev("s_sel")
            s_pos = ev("s_pos")
            s_put = [ev(f"s_put{q}") for q in range(8)]
            s_ini = ev("s_ini")
            s_w2 = ev("s_w2")
            s_ix = ev("s_ix")
            s_rows = [ev(f"s_rows{q}") for q in range(GU)]
            s_ohr = ev("s_ohr")
            s_used = ev("s_used")
            s_sum = ev("s_sum")
            s_mean = ev("s_mean")
            s_st = ev("s_st")
            s_stc = ev("s_stc")
            s_xl = [ev(f"s_xlc{u}") for u in range(2)]
            s_lin = ev("s_lin")
            s_nrm = ev("s_nrm")
            s_x1 = ev("s_x1")
            s_std = ev("s_stdc")
            s_x2 = ev("s_x2")
            s_x2p = ev("s_x2p")
            s_x2c = ev("s_x2c")
            s_h = ev("s_h")
            s_hc = ev("s_hc")
            s_x1s = [ev(f"s_x1s{u}") for u in range(2)]
            s_x2s = [ev(f"s_x2s{u}") for u in range(2)]
            s_rts = [ev(f"s_rts{u}") for u in range(2)]
            s_pr = ev("s_pr")

            def first_chunk(c):
                return nc.s_assert_within(c, 0, GC, skip_runtime_bounds_check_because=
                                          "a tile's rounds end at most GU - 1 chunks past its last chunk")

            def plan(eng, t):
                return (eng.value_load(gplan[0:1, bass.ds(t, 1)], min_val=0, max_val=GC - 1),
                        eng.value_load(gplan[0:1, bass.ds(t + NT, 1)], min_val=0, max_val=GC // GU + 1),
                        eng.value_load(gplan[0:1, bass.ds(t + 2 * NT, 1)], min_val=0, max_val=NT * (GC // GU + 1)))

            @block.sync
            def _(sp):
                sp.wait_ge(s_ini, 1)
                sp.dma_start(route_rows[N:N + 1, :], pad_row[:]).then_inc(s_pr, 16)

                def edges(i):
                    for h in range(2):
                        sp.wait_ge(s_blf, i * 2 + (h + 1))
                        c = i * 8 + 4 * h
                        sp.dma_start(dst_b[h][:], to_all(fedge[1:2, bass.ds(c * P, 4 * P)])).then_inc(s_bl[h], 16)
                        sp.dma_start(hi_bc[h][:], to_all(hi_rows[bass.ds(c, 4), :].rearrange("(o c) e -> o (c e)", o=1))).then_inc(s_bl[h], 16)

                with sp.Fori(0, PRE + 1) as i:
                    edges(i)
                for e in range(NE):
                    sp.dma_start(w2_sb[:, e, :, :], w2[e].rearrange("(k p) f -> p k f", p=P)).then_inc(s_w2, 16)

                def load(t, u):
                    sp.wait_ge(s_x2, t + 1)
                    sp.dma_start(x_in[u][:], x[bass.ds(t * NP, NP), :]).then_inc(s_xl[u], 16)
                    sp.dma_start(x_t[u][:], xn_turned[bass.ds(t, 1), :, :].rearrange("o p c -> p (o c)")).then_inc(s_xl[u], 16)

                def store_x1(t, u):
                    sp.wait_ge(s_x2, t + 3)
                    sp.dma_start(x1_rows[bass.ds(t * NP, NP), :], x1[u][:]).then_inc(s_x1s[u], 16)

                def store_x2(t, u):
                    sp.wait_ge(s_x2c, t + 2)
                    sp.dma_start(x2_turned[bass.ds(t, 1), :, :].rearrange("o p c -> p (o c)"), x2_t[u][:]).then_inc(s_x2s[u], 16)

                def store_rt(t, u):
                    sp.wait_ge(s_hc, t + 2)
                    sp.dma_start(route_rows[bass.ds(t * NP, NP), :], rt[u][:]).then_inc(s_rts[u], 16)

                steps(sp, NT, 2, [(0, lambda t, u: edges(t + (PRE + 1))), (1, load), (3, store_x1), (4, store_x2), (6, store_rt)])
                for u in range(2):
                    for s in (s_x1s, s_x2s, s_rts):
                        sp.wait_ge(s[u], 16 * NT // 2)
                sp.wait_ge(s_pr, 16)
                sp.wait_ge(s_w2, NE * 16)

            @block.gpsimd
            def _(pool):
                def gather(t, u):
                    c0, rounds, before = plan(pool, t)
                    def one_round(g):
                        k = g + before
                        c = first_chunk(c0 + g * GU)
                        for part, (q, end) in enumerate(((0, 5), (5, GU))):
                            pool.wait_ge(s_used, k * GU + end)
                            pool.sem_inc(s_gate, 1)
                            nc.gpsimd.tensor_copy(idx[:, q:end], gsrc[:, bass.ds(c + q, end - q)]).then_inc(s_ix, 1)
                            pool.wait_ge(s_ix, k * 2 + (part + 1))
                            pool.sem_inc(s_gate, 1)
                            for r in range(q, end):
                                pool.indirect_dma_start(out=rows[:, r, 0:D], out_offset=None, in_=xn_rows,
                                                        in_offset=bass.IndirectOffsetOnAxis(ap=idx[:, r:r + 1], axis=0)
                                                        ).then_inc(s_rows[r], 16)

                    repeat(pool, rounds, one_round)
                def scatter(i):
                    for h in range(2):
                        pool.wait_ge(s_pos, i * 2 + (h + 1))
                        pool.sem_inc(s_gate, 1)
                        for q in range(4 * h, 4 * h + 4):
                            pool.indirect_dma_start(
                                out=lists, out_offset=bass.IndirectOffsetOnAxis(ap=pos_i[:, q:q + 1], axis=0),
                                in_=val_i[:, q:q + 1], in_offset=None).then_inc(s_put[q], 16)

                with pool.Fori(0, PRE) as i:
                    scatter(i)
                with pool.Fori(0, NT) as t:
                    gather(t, 0)
                    scatter(t + PRE)
                scatter(PRE + NT)
                for q in range(8):
                    pool.wait_ge(s_put[q], 16 * FC // 8)

            @block.vector
            def _(dve):
                v = nc.vector
                v.memset(rows[:, :, D:D + 1], 1.0)
                v.memset(pad_row[:, 0:20], 0.0)
                v.memset(pad_row[:, 20:ROW], NEG)
                for u in range(2):
                    v.memset(rt[u][:], 1.0)
                v.drain()
                dve.sem_inc(s_ini, 1)
                dve.sem_inc(s_mean, 2)
                dve.sem_inc(s_x1, 1)
                dve.sem_inc(s_x2, 2)
                dve.sem_inc(s_hc, 1)
                dve.sem_inc(s_blf, 2)
                dve.sem_inc(s_sel, 2)
                def prepare(i, h):
                    dve.wait_ge(s_bl[h], i * 32 + 32)
                    wait_after(dve, s_cnt, i * 8 + (4 * h - 4))
                    v.tensor_scalar(oh_t[h][:], hi_bc[h][0:NT, :], iota_p[0:NT, :], None, ALU.is_equal).then_inc(s_oht, 1)
                    for to, of, n in ((oh_hi, hi_e, NT), (oh_lo, lo_e, NP)):
                        last = v.tensor_tensor(to[:, 4 * h:4 * h + 4, :],
                                               iota_j[:, 0:n].rearrange("p (o n) -> p o n", o=1).broadcast_to([P, 4, n]),
                                               along(of[:, bass.ds(i * 8 + 4 * h, 4)], n), ALU.is_equal)
                    last.then_inc(s_oh, 1)
                    for q in range(4 * h, 4 * h + 4):
                        e = (q % 4) * P
                        last = v.scalar_tensor_tensor(out=junk[:, q, :], in0=dst_b[h][:, e:e + P], scalar=dst_e[:, bass.ds(i * 8 + q, 1)],
                                                      in1=below[:], op0=ALU.is_equal, op1=ALU.mult, accum_out=rk[:, q:q + 1])
                    last.then_inc(s_blf, 1)

                def select(i, h):
                    cols, s4 = bass.ds(i * 8 + 4 * h, 4), slice(4 * h, 4 * h + 4)
                    dve.wait_ge(s_look, i * 2 + (h + 1))
                    for q in range(4 * h, 4 * h + 4):
                        at_q = LOOK[h][:, (q % 4) * NP:(q % 4 + 1) * NP]
                        last = v.scalar_tensor_tensor(out=junk_l[:, q, 0:NP], in0=iota_j[:, 0:NP], scalar=lo_e[:, bass.ds(i * 8 + q, 1)],
                                                      in1=at_q, op0=ALU.is_equal, op1=ALU.mult, accum_out=tv[:, q:q + 1])
                    last.then_inc(s_sel, 1)
                    v.drain()
                    v.tensor_tensor(tv[:, s4], tv[:, s4], rk[:, s4], ALU.add)
                    v.drain()
                    v.tensor_scalar(blk_f[:, s4], tv[:, s4], 1.0 / FU, -(FU - 1) / (2.0 * FU), ALU.mult, ALU.add)
                    v.scalar_tensor_tensor(out=pos_f[:, s4], in0=lo_e[:, cols], scalar=float(FU), in1=tv[:, s4], op0=ALU.mult, op1=ALU.add)
                    v.drain()
                    v.tensor_scalar(blk_f[:, s4], blk_f[:, s4], MAGIC, MAGIC, ALU.add, ALU.subtract)
                    v.drain()
                    for q in range(4 * h, 4 * h + 4):
                        wait_after(dve, s_put[q], i * 16)
                    v.scalar_tensor_tensor(out=pos_i[:, s4], in0=blk_f[:, s4], scalar=float(BLK - FU), in1=pos_f[:, s4], op0=ALU.mult, op1=ALU.add)
                    v.tensor_copy(val_i[:, s4], src_e[:, cols]).then_inc(s_pos, 1)

                def place(i, last=False):
                    for h in range(2):
                        select(i, h)
                        if not last:
                            prepare(i + 1, h)

                prepare(0, 0)
                prepare(0, 1)
                place(0)
                with dve.Fori(1, PRE) as i:
                    place(i)

                def one_hot(t, u):
                    c0, rounds, before = plan(dve, t)
                    def one_round(g):
                        k = g + before
                        c = first_chunk(c0 + g * GU)
                        for q in range(GU):
                            dve.wait_ge(s_used, k * GU + (q + 1))
                            v.tensor_scalar(oh[:, q, :], iota_j[:, 0:NP], gdst[:, bass.ds(c + q, 1)],
                                            neg_first[:, bass.ds(t, 1)], ALU.subtract, ALU.is_equal).then_inc(s_ohr, 1)

                    repeat(dve, rounds, one_round)
                def mean(t, u):
                    dve.wait_ge(s_sum, t + 1)
                    v.tensor_scalar(rdeg[u][:], SUM[u][0:NP, D:D + 1], 1.0, None, ALU.max)
                    v.drain()
                    v.reciprocal(rdeg[u][:], rdeg[u][:])
                    v.drain()
                    v.tensor_scalar(s_sb[u][:], SUM[u][0:NP, 0:D], rdeg[u][:], None, ALU.mult).then_inc(s_mean, 1)

                def residual(t, u):
                    dve.wait_ge(s_nrm, t + 1)
                    dve.wait_ge(s_xl[u], (t - u) * 16 + 32)
                    wait_after(dve, s_x1s[u], (t - u) * 8)
                    v.reciprocal(ssq[u][:], ssq[u][:])
                    v.drain()
                    v.scalar_tensor_tensor(out=x1[u][:], in0=G, scalar=ssq[u][:], in1=x_in[u][:], op0=ALU.mult, op1=ALU.add)
                    v.drain()
                    v.tensor_tensor(x1[u][:], x1[u][:], MX, ALU.add)
                    v.drain()
                    v.tensor_tensor(x1[u][:], x1[u][:], bias_x[0:NP, :], ALU.add)
                    v.drain()
                    v.bn_stats(st6[u][:], x1[u][:])
                    v.drain()
                    v.bn_aggr(mv[u][:], st6[u][:]).then_inc(s_x1, 1)

                def second_norm(t, u):
                    dve.wait_ge(s_std, t + 1)
                    v.reciprocal(rstd[u][:], rstd[u][:])
                    v.drain()
                    v.tensor_scalar(x2[u][:], x1[u][:], mv[u][:, 0:1], rstd[u][:], ALU.subtract, ALU.mult).then_inc(s_x2, 1)

                def router_row(t, u):
                    dve.wait_ge(s_h, t + 1)
                    wait_after(dve, s_rts[u], (t - u) * 8)
                    v.tensor_copy(rt[u][:, 0:20].rearrange("p (h e) -> p h e", e=5)[:, :, 0:4],
                                  H[0:NP, 0:16].rearrange("p (h e) -> p h e", e=4))
                    v.tensor_copy(adst[:, bass.ds(t, 1), :].rearrange("p o h -> p (o h)"), H[0:NP, 20:24])
                    v.tensor_copy(rt[u][:, 20:24], H[0:NP, 16:20]).then_inc(s_hc, 1)

                steps(dve, NT, 2, [(0, one_hot), (6, router_row), (1, mean), (3, residual), (3, second_norm),
                                   (0, lambda t, u: place(t + PRE))])
                place(PRE + NT, last=True)

            @block.scalar
            def _(act):
                a = nc.scalar.activation
                act.sem_inc(s_stc, 1)
                act.sem_inc(s_x2c, 1)
                act.sem_inc(s_tab, 1)

                def tables(i):
                    for q in range(8):
                        act.wait_ge(s_cnt, i * 8 + (q + 1))
                        a(t_sb[(q + 1) % 2][:], CNT[0:NT, 0:NP], ACT.Identity, bias=base8[0:NT, :]).then_inc(s_tab, 1)

                def turn_mean(t, u):
                    act.wait_ge(s_st, t + 1)
                    a(s_t[u][:], ST, ACT.Copy).then_inc(s_stc, 1)

                def norms(t, u):
                    act.wait_ge(s_lin, t + 1)
                    a(sq[u][:], G, ACT.Square, accum_out=ssq[u][:])
                    act.drain()
                    a(ssq[u][:], ssq[u][:], ACT.Sqrt).then_inc(s_nrm, 1)

                def std(t, u):
                    act.wait_ge(s_x1, t + 2)
                    a(rstd[u][:], mv[u][:, 1:2], ACT.Sqrt, bias=eps_c[0:NP, :]).then_inc(s_std, 1)

                def turn_x2(t, u):
                    act.wait_ge(s_x2p, t + 1)
                    act.wait_ge(s_st, min(t + 4, NT) if isinstance(t, int) else t + 4)
                    wait_after(act, s_x2s[u], (t - u) * 8)
                    a(x2_t[u][:], X2, ACT.Copy).then_inc(s_x2c, 1)

                with act.Fori(0, PRE) as i:
                    tables(i)
                steps(act, NT, 2, [(0, lambda t, u: tables(t + PRE)), (3, std), (4, turn_x2), (1, turn_mean), (2, norms)])
                tables(PRE + NT)

            @block.tensor
            def _(pe):
                mm = nc.tensor.matmul
                pe.sem_inc(s_used, GU)

                def look_up(i):
                    for h in range(2):
                        pe.wait_ge(s_oht, i * 2 + (h + 1))
                        pe.wait_ge(s_oh, i * 2 + (h + 1))
                        pe.wait_ge(s_sel, i * 2 + (h + 1))
                        for q in range(4 * h, 4 * h + 4):
                            cols = slice((q % 4) * NP, (q % 4 + 1) * NP)
                            pe.wait_ge(s_tab, i * 8 + (q + 1))
                            mm(CNT[0:NT, 0:NP], oh_hi[:, q, :], oh_lo[:, q, :], start=False, stop=True, skip_group_check=True).then_inc(s_cnt, 1)
                            last = mm(LOOK[h][:, cols], oh_t[h][:, (q % 4) * P:(q % 4 + 1) * P], t_sb[q % 2][:], start=True, stop=True)
                            if q % 4 == 3:
                                last.then_inc(s_look, 1)

                def sums(t, u):
                    _, rounds, before = plan(pe, t)
                    look_up(t + PRE)
                    pe.wait_ge(s_mean, t + 1)
                    mm(SUM[u][0:NP, 0:D + 1], zeros_b[:, 0:NP], zeros_b[:, 0:D + 1], start=True, stop=False)
                    def one_round(g):
                        k = g + before
                        for q in range(GU):
                            pe.wait_ge(s_rows[q], k * 16 + 16)
                            pe.wait_ge(s_ohr, k * GU + (q + 1))
                            mm(SUM[u][0:NP, 0:D + 1], oh[:, q, :], rows[:, q, :], start=False, stop=False).then_inc(s_used, 1)
                    repeat(pe, rounds, one_round)
                    mm(SUM[u][0:NP, 0:D + 1], zeros_b[:, 0:NP], zeros_b[:, 0:D + 1], start=False, stop=True).then_inc(s_sum, 1)

                def turn_mean(t, u):
                    pe.wait_ge(s_mean, t + 3)
                    pe.wait_ge(s_stc, t + 1)
                    for k in range(2):
                        last = nc.tensor.transpose(ST[:, k * NP:(k + 1) * NP], s_sb[u][:, k * P:(k + 1) * P], ident[0:NP, 0:NP])
                    last.then_inc(s_st, 1)

                def linear(t, u):
                    pe.wait_ge(s_stc, t + 2)
                    pe.wait_ge(s_xl[u], (t - u) * 16 + 32)
                    pe.wait_ge(s_x1, t + 1)
                    for k in range(2):
                        xk = x_t[u][:, k * NP:(k + 1) * NP]
                        mm(G, xk, wg[:, k, :], start=k == 0, stop=False)
                        mm(G, s_t[u][:, k * NP:(k + 1) * NP], wg[:, 2 + k, :], start=False, stop=k == 1)
                    for k in range(2):
                        last = mm(MX, x_t[u][:, k * NP:(k + 1) * NP], mix[:, k, :], start=k == 0, stop=k == 1)
                    last.then_inc(s_lin, 1)

                def turn_x2(t, u):
                    pe.wait_ge(s_x2, t + 3)
                    pe.wait_ge(s_x2c, t + 1)
                    pe.wait_ge(s_stc, min(t + 4, NT + 1) if isinstance(t, int) else t + 4)
                    for k in range(2):
                        last = nc.tensor.transpose(X2[:, k * NP:(k + 1) * NP], x2[u][:, k * P:(k + 1) * P], ident[0:NP, 0:NP])
                    last.then_inc(s_x2p, 1)

                def router(t, u):
                    pe.wait_ge(s_x2c, t + 2)
                    pe.wait_ge(s_hc, t + 1)
                    for k in range(2):
                        last = mm(H[0:NP, 0:ROW], x2_t[u][:, k * NP:(k + 1) * NP], wr[:, k, :], start=k == 0, stop=k == 1)
                    last.then_inc(s_h, 1)

                with pe.Fori(0, PRE) as i:
                    look_up(i)
                steps(pe, NT, 2, [(0, sums), (5, router), (4, turn_x2), (1, turn_mean), (2, linear)])
                look_up(PRE + NT)

        with ExitStack() as stage, nc.Block() as block:
            one = lambda name, shape, dt=f32: stage.enter_context(nc.sbuf_tensor(name, shape, dt))
            two = lambda name, shape, dt=f32: [one(f"{name}{u}", shape, dt) for u in range(2)]
            ev = lambda name: stage.enter_context(nc.semaphore(name))
            b1_sb, b2_sb = one("b1_sb", [P, 16]), one("b2_sb", [1, NE * D])
            bg, lg, lb = one("bg", [NP, 16]), one("lg", [NP, 16]), one("lb", [NP, 16])
            first_e = one("first_e", [NP, 4, 4])
            ix = one("ix", [NP, RING, FU], i32)
            nb_rows = one("nb_rows", [NP, RING, FU + 2, ROW])
            lk, dif, pr, msg = (one(n, [NP, k, m]) for n, k, m in
                                (("lk", FU + 2, 4), ("dif", FU + 1, 4), ("pr", FU + 1, 4), ("msg", FU + 1, 20)))
            own, ad = one("own", [NP, 4, ROW]), one("ad", [NP, 4])
            res = one("res", [NP, 4, ROW])
            rden, agg, asq = one("rden", [NP, 4, 4]), one("agg", [NP, 4, 16]), one("asq", [NP, 4, 16])
            m4, v4 = one("m4", [NP, 4]), one("v4", [NP, 4])
            sc, sx, gt, eq = one("sc", [NP, 4, 4]), one("sx", [NP, 4, 4]), one("gt", [NP, 4, 4, 4]), one("eq", [NP, 4, 4, 4])
            rank = one("rank", [NP, 4, 4])
            gate = two("gate", [NP, 4, 4])
            ones = one("ones", [1, NP])
            x2g = two("x2g", [P, 2, 4, NP])
            hid = two("hid", [P, 16, 4 * NP])
            x1g, acc = two("x1g", [NP, 4, D]), two("acc", [NP, 4, D])
            HP, Y0, Y1 = PS[0:4], PS[4:6], PS[6:8]
            s_pl = ev("s_pl")
            s_w1 = ev("s_w1")
            s_fe = ev("s_fe")
            s_ones = ev("s_ones")
            s_ld = [ev(f"s_ld{h}") for h in range(2)]
            s_nb = [ev(f"s_nbr{r}") for r in range(RING)]
            s_blk = ev("s_blk")
            s_free = ev("s_free")
            s_own = [ev(f"s_own{j}") for j in range(4)]
            s_ownf = ev("s_ownf")
            s_dif = ev("s_dif")
            s_pr = ev("s_prob")
            s_var = ev("s_varf")
            s_rt = ev("s_rtf")
            s_ex = ev("s_ex")
            s_exd = ev("s_exd")
            s_x2l = [ev(f"s_x2l{u}") for u in range(2)]
            s_x1l = [[ev(f"s_x1l{u}{j}") for j in range(4)] for u in range(2)]
            s_hp = ev("s_hp")
            s_hid = ev("s_hid")
            s_y = ev("s_y")
            s_acc = ev("s_acc")
            s_out = [[ev(f"s_out{u}{j}") for j in range(4)] for u in range(2)]

            def list_plan(eng, t):
                return (eng.value_load(fplan[0:1, bass.ds(t, 1)], min_val=0, max_val=EF // FU + 1),
                        eng.value_load(fplan[0:1, bass.ds(t + NT, 1)], min_val=0, max_val=LIST_BLOCKS))

            def all_blocks(eng):
                return (eng.value_load(fplan[0:1, NT - 1:NT], min_val=0, max_val=EF // FU + 1) +
                        eng.value_load(fplan[0:1, 2 * NT - 1:2 * NT], min_val=0, max_val=LIST_BLOCKS))

            def block_no(b):
                return nc.s_assert_within(b, 0, LIST_BLOCKS - 1, skip_runtime_bounds_check_because=
                                          "LIST_BLOCKS covers the blocks of any edges")

            @block.sync
            def _(sp):
                for to, of in ((b1_sb[:], b1), (b2_sb[:], b2.rearrange("(o e) f -> o (e f)", o=1)), (bg[:], row_of(b_gat, 16)), (lg[:], row_of(ln_g, 16)),
                               (lb[:], row_of(ln_b, 16))):
                    sp.dma_start(to, of).then_inc(s_pl, 16)
                for e in range(NE):
                    sp.dma_start(w1_sb[:, :, e, :], w1[e].rearrange("(k p) f -> p k f", p=P)).then_inc(s_w1, 16)
                def group(g, u):
                    for j in range(4):
                        t, nth = g + NG * j, g * 4 + j
                        if j == 0:
                            sp.wait_ge(s_hp, g * 16)
                            for i in range(4):
                                sp.dma_start(x2g[u][:, :, i, :], x2_turned[bass.ds(t + NG * i, 1), :, :]
                                             .rearrange("o p (k n) -> p (o k) n", k=2)).then_inc(s_x2l[u], 16)
                        sp.wait_ge(s_acc, nth + 1)
                        sp.dma_start(x1g[u][:, j, :], x1_rows[bass.ds(t * NP, NP), :]).then_inc(s_x1l[u][j], 16)
                        sp.wait_ge(s_ownf, nth + 1)
                        sp.dma_start(own[:, j, :], route_rows[bass.ds(t * NP, NP), :]).then_inc(s_own[j], 16)
                def store(g, u):
                    for j in range(4):
                        t = g + NG * j
                        sp.wait_ge(s_acc, g * 4 + (j + 9))
                        sp.dma_start(out[bass.ds(t * NP, NP), :], acc[u][:, j, :]).then_inc(s_out[u][j], 16)

                steps(sp, NG, 2, [(0, group), (2, store)])
                for u in range(2):
                    for j in range(4):
                        sp.wait_ge(s_out[u][j], 16 * ((NG + 1 - u) // 2))
                for u in range(4):
                    sp.wait_ge(s_own[u], 16 * NG)

            @block.gpsimd
            def _(pool):
                nc.gpsimd.memset(first_e[:], 1.0).then_inc(s_fe, 1)
                pool.wait_ge(s_fe, 1)
                nc.gpsimd.affine_select(out=first_e[:], in_=first_e[:], compare_op=ALU.is_gt, fill=0.0, base=0,
                                        pattern=[[1, 4], [-1, 4]], channel_multiplier=0).then_inc(s_fe, 1)
                HALF = RING // 2

                def load(i, h):
                    pool.dma_start(ix[:, h * HALF:(h + 1) * HALF, :],
                                   lists[bass.ds(i * (RING * BLK) + h * (HALF * BLK), HALF * BLK), :]
                                   .rearrange("(r p c) o -> p r (c o)", p=NP, c=FU)).then_inc(s_ld[h], 16)

                def fetch(i, r):
                    if r % HALF == 0:
                        pool.wait_ge(s_ld[r // HALF], i * 16 + 16)
                        pool.sem_inc(s_gate, 1)
                    pool.wait_ge(s_free, i * RING + (r + 1))
                    pool.sem_inc(s_gate, 1)
                    for q in range(FU):
                        pool.indirect_dma_start(out=nb_rows[:, r, q, :], out_offset=None, in_=route_rows,
                                                in_offset=bass.IndirectOffsetOnAxis(ap=ix[:, r, q:q + 1], axis=0)
                                                ).then_inc(s_nb[r], 16)

                def announce(i, r):
                    pool.wait_ge(s_nb[r], i * (16 * FU) + 16 * FU)
                    pool.sem_inc(s_blk, 1)

                def ring_round(i, first):
                    for r in range(RING):
                        fetch(i, r)
                        if r:
                            announce(i, r - 1)
                        elif not first:
                            announce(i - 1, RING - 1)
                            load(i, 1)
                        if r == HALF:
                            load(i + 1, 0)

                def all_rounds():
                    rounds = nc.s_assert_within((all_blocks(pool) + (RING - 1)) // RING, 1, LIST_BLOCKS // RING - 1,
                                                skip_runtime_bounds_check_because="there is an edge, so there is a round")
                    load(0, 0)
                    load(0, 1)
                    ring_round(0, True)
                    repeat(pool, rounds - 1, lambda i: ring_round(i + 1, False))
                    announce(rounds - 1, RING - 1)
                    pool.wait_ge(s_ld[0], rounds * 16 + 16)

                all_rounds()

            @block.vector
            def _(dve):
                v = nc.vector
                v.memset(ones[:], 1.0).then_inc(s_ones, 1)
                dve.sem_inc(s_free, RING)
                dve.sem_inc(s_ownf, 4)
                dve.sem_inc(s_acc, 8)
                dve.wait_ge(s_pl, 5 * 16)
                dve.wait_ge(s_fe, 2)

                def slot_of(k, r0, r1, c0, c1):
                    return nb_rows[:, bass.ds(k % RING, 1), r0:r1, c0:c1].rearrange("p o r c -> p (o r) c")

                def attend(g, j):
                    t = g + NG * j
                    dve.wait_ge(s_own[j], g * 16 + 16)
                    blocks, before = list_plan(dve, t)
                    v.tensor_copy(slot_of(before, FU, FU + 1, 0, ROW), own[:, j:j + 1, :]).then_inc(s_ownf, 1)
                    v.tensor_copy(ad[:], adst[:, bass.ds(t, 1), :].rearrange("p o h -> p (o h)"))
                    v.drain()
                    def one_block(b):
                        k = block_no(b + before)
                        rows = lambda r0, r1, c0, c1: slot_of(k, r0, r1, c0, c1)
                        nxt = lambda c0, c1: slot_of(k + 1, FU, FU + 1, c0, c1)
                        dve.wait_ge(s_blk, k + 1)
                        v.tensor_reduce(rows(FU + 1, FU + 2, 20, 24), rows(0, FU + 1, 20, 24).rearrange("p r h -> p h r"), AX.X, ALU.max)
                        v.drain()
                        v.tensor_tensor(lk[:], rows(0, FU + 2, 20, 24), ad[:].rearrange("p (o h) -> p o h", o=1).broadcast_to([NP, FU + 2, 4]), ALU.add)
                        v.tensor_copy(nxt(20, 24), rows(FU + 1, FU + 2, 20, 24))
                        v.drain()
                        v.scalar_tensor_tensor(out=lk[:], in0=lk[:], scalar=0.2, in1=lk[:], op0=ALU.mult, op1=ALU.max)
                        v.drain()
                        v.tensor_tensor(dif[:], lk[:, 0:FU + 1, :], lk[:, FU + 1:FU + 2, :].broadcast_to([NP, FU + 1, 4]), ALU.subtract).then_inc(s_dif, 1)
                        dve.wait_ge(s_pr, k + 1)
                        v.tensor_tensor(msg[:].rearrange("p r (h e) -> p r h e", e=5),
                                        rows(0, FU + 1, 0, 20).rearrange("p r (h e) -> p r h e", e=5),
                                        pr[:].rearrange("p r (h o) -> p r h o", o=1).broadcast_to([NP, FU + 1, 4, 5]), ALU.mult)
                        v.drain()
                        v.tensor_reduce(nxt(0, 20).rearrange("p o c -> p (o c)"), msg[:].rearrange("p r c -> p c r"), AX.X, ALU.add)
                        v.drain()
                        dve.sem_inc(s_free, 1)
                    repeat(dve, blocks, one_block)
                    v.tensor_copy(res[:, j:j + 1, :], slot_of(before + blocks, FU, FU + 1, 0, ROW))
                    v.drain()

                def weigh(g, u):
                    q5 = res[:, :, 0:20].rearrange("p t (h e) -> p t h e", e=5)
                    by_head = lambda a: a[:].rearrange("p t (h e) -> p t h e", e=4)
                    bc = lambda a: a[:].rearrange("p (o c) -> p o c", o=1).broadcast_to([NP, 4, 16])
                    v.tensor_scalar(rden[:].rearrange("p t (h o) -> p t h o", o=1), q5[:, :, :, 4:5], 1e-16, None, ALU.add)
                    v.drain()
                    v.reciprocal(rden[:], rden[:])
                    v.drain()
                    v.tensor_tensor(by_head(agg), q5[:, :, :, 0:4],
                                    rden[:].rearrange("p t (h o) -> p t h o", o=1).broadcast_to([NP, 4, 4, 4]), ALU.mult)
                    v.drain()
                    v.tensor_tensor(agg[:], agg[:], bc(bg), ALU.add)
                    v.drain()
                    v.tensor_reduce(m4[:], agg[:], AX.X, ALU.add)
                    v.drain()
                    v.tensor_scalar(m4[:], m4[:], 1.0 / 16, None, ALU.mult)
                    v.drain()
                    v.tensor_tensor(agg[:], agg[:], along(m4[:], 16), ALU.subtract)
                    v.drain()
                    v.tensor_tensor(asq[:], agg[:], agg[:], ALU.mult)
                    v.drain()
                    v.tensor_reduce(v4[:], asq[:], AX.X, ALU.add).then_inc(s_var, 1)
                    dve.wait_ge(s_rt, g + 1)
                    v.reciprocal(v4[:], v4[:])
                    v.drain()
                    v.tensor_tensor(agg[:], agg[:], along(v4[:], 16), ALU.mult)
                    v.drain()
                    v.tensor_tensor(agg[:], agg[:], bc(lg), ALU.mult)
                    v.drain()
                    v.tensor_tensor(agg[:], agg[:], bc(lb), ALU.add)
                    v.drain()
                    v.tensor_reduce(sc[:], agg[:].rearrange("p t (h e) -> p t e h", e=4), AX.X, ALU.add)
                    v.drain()
                    v.tensor_scalar(sc[:], sc[:], 0.25, None, ALU.mult)
                    v.drain()
                    other = sc[:].rearrange("p t (o j) -> p t o j", o=1).broadcast_to([NP, 4, 4, 4])
                    this = sc[:].rearrange("p t (e o) -> p t e o", o=1).broadcast_to([NP, 4, 4, 4])
                    v.tensor_tensor(gt[:], other, this, ALU.is_gt)
                    v.tensor_tensor(eq[:], other, this, ALU.is_equal)
                    v.tensor_reduce(m4[:], sc[:], AX.X, ALU.max)
                    v.drain()
                    for t in range(4):
                        v.tensor_tensor(eq[:, t, :, :], eq[:, t, :, :], first_e[:], ALU.mult)
                    v.tensor_tensor(sx[:], sc[:], along(m4[:], 4), ALU.subtract).then_inc(s_ex, 1)
                    v.drain()
                    v.tensor_tensor(gt[:], gt[:], eq[:], ALU.add)
                    v.drain()
                    v.tensor_reduce(rank[:], gt[:], AX.X, ALU.add)
                    v.drain()
                    dve.wait_ge(s_exd, g + 1)
                    v.scalar_tensor_tensor(out=sx[:], in0=rank[:], scalar=1.5, in1=sx[:], op0=ALU.is_lt, op1=ALU.mult)
                    v.drain()
                    v.tensor_reduce(m4[:], sx[:], AX.X, ALU.add)
                    v.drain()
                    v.reciprocal(m4[:], m4[:])
                    v.drain()
                    v.tensor_tensor(gate[u][:], sx[:], along(m4[:], 4), ALU.mult)
                    v.drain()

                def combine(g, u, j):
                    dve.wait_ge(s_x1l[u][j], (g - u) * 8 + 16)
                    wait_after(dve, s_out[u][j], (g - u) * 8)
                    dve.wait_ge(s_y, g * 4 + (j + 1))
                    Y = Y1 if j % 2 else Y0
                    for e in range(NE):
                        if e:
                            v.drain()
                        last = v.scalar_tensor_tensor(out=acc[u][:, j, :], in0=Y[e // 2][0:NP, (e % 2) * D:(e % 2 + 1) * D],
                                                      scalar=gate[u][:, j, e:e + 1], in1=(acc if e else x1g)[u][:, j, :], op0=ALU.mult, op1=ALU.add)
                    last.then_inc(s_acc, 1)

                steps(dve, NG, 2, [s for j in range(4) for s in (
                    (0, lambda g, u, j=j: attend(g, j)), (1, lambda g, u, j=j: combine(g, u, j)))] + [(0, weigh)])

            @block.scalar
            def _(act):
                a = nc.scalar.activation
                act.sem_inc(s_hid, 4)

                def gelus(g, u, e):
                    for c in range(4 * e, 4 * e + 4):
                        act.wait_ge(s_hp, g * 16 + (c + 17))
                        a(hid[u][:, c, :], HP[c % 4][:, 0:4 * NP], ACT.Gelu, bias=b1_sb[:, c:c + 1]).then_inc(s_hid, 1)

                def exps(g, j):
                    blocks, before = list_plan(act, g + NG * j)
                    def one_block(b):
                        k = block_no(b + before)
                        act.wait_ge(s_dif, k + 1)
                        a(pr[:], dif[:], ACT.Exp).then_inc(s_pr, 1)

                    repeat(act, blocks, one_block)
                def weigh(g, u):
                    act.wait_ge(s_var, g + 1)
                    a(v4[:], v4[:], ACT.Sqrt, bias=eps_c[0:NP, :], scale=1.0 / 16).then_inc(s_rt, 1)
                    act.wait_ge(s_ex, g + 1)
                    a(sx[:], sx[:], ACT.Exp).then_inc(s_exd, 1)

                act.wait_ge(s_pl, 5 * 16)
                steps(act, NG, 2, [s for j in range(4) for s in (
                    (0, lambda g, u, j=j: exps(g, j)), (0, lambda g, u, j=j: gelus(g, u, j)))] + [(0, weigh)])

            @block.tensor
            def _(pe):
                mm = nc.tensor.matmul
                pe.sem_inc(s_hp, 16)
                pe.wait_ge(s_pl, 5 * 16)
                pe.wait_ge(s_w1, NE * 16)
                pe.wait_ge(s_ones, 1)

                def outputs(g, u, j):
                    if j == 0:
                        pe.wait_ge(s_hid, g * 16 + 20)
                    pe.wait_ge(s_acc, g * 4 + (j + 7))
                    Y = Y1 if j % 2 else Y0
                    for e in range(NE):
                        for k in range(4):
                            mm(Y[e // 2][0:NP, (e % 2) * D:(e % 2 + 1) * D], hid[u][:, 4 * e + k, j * NP:(j + 1) * NP],
                               w2_sb[:, e, k, :], start=k == 0, stop=False)
                        last = mm(Y[e // 2][0:NP, (e % 2) * D:(e % 2 + 1) * D], ones[:], b2_sb[:, e * D:(e + 1) * D], start=False, stop=True)
                    last.then_inc(s_y, 1)

                def hidden(g, u, e):
                    if e == 0:
                        pe.wait_ge(s_x2l[u], (g - u) * 32 + 64)
                    for c in range(4 * e, 4 * e + 4):
                        pe.wait_ge(s_hid, g * 16 + (c + 1))
                        for k in range(2):
                            last = mm(HP[c % 4][:, 0:4 * NP], w1_sb[:, k, e, (c % 4) * P:(c % 4 + 1) * P],
                                      x2g[u][:, k, :, :].rearrange("p j n -> p (j n)"), start=k == 0, stop=k == 1)
                        last.then_inc(s_hp, 1)

                steps(pe, NG, 2, [s for j in range(4) for s in (
                    (1, lambda g, u, j=j: outputs(g, u, j)), (0, lambda g, u, j=j: hidden(g, u, j)))])



_INS = ["x", "src", "dst", "L0_gnn_weight", "L0_gnn_bias", "L0_mix_Wqkv", "kv_turned", "out_turned", "L0_mix_bout",
        "L0_ffn_W_gat", "L0_ffn_att_src", "L0_ffn_att_dst", "L0_ffn_b_gat", "L0_ffn_ln_gamma", "L0_ffn_ln_beta",
        "L0_ffn_W1", "b1_cols", "L0_ffn_W2", "L0_ffn_b2", "L0_ffn_edge_index"]


def kernel(**inputs):
    import numpy as np
    import concourse.bacc as bacc
    from concourse.bass_utils import run_bass_kernel_spmd

    given = {k: np.asarray(v) for k, v in inputs.items()}
    given["kv_turned"] = given["L0_mix_Wqkv"][INNER:].T
    given["out_turned"] = given["L0_mix_Wout"].T
    given["b1_cols"] = given["L0_ffn_b1"].reshape(NE * 4, P).T
    nc = bacc.Bacc("TRN2", target_bir_lowering=False, num_devices=1)
    arrays, args = {}, []
    for name in _INS:
        a = np.ascontiguousarray(given[name])
        arrays[f"in_{name}"] = a
        args.append(nc.dram_tensor(f"in_{name}", a.shape, mybir.dt.from_np(a.dtype), kind="ExternalInput").ap())
    args.append(nc.dram_tensor("out", (N, D), f32, kind="ExternalOutput").ap())
    build(nc, *args)
    r = run_bass_kernel_spmd(nc, [arrays], core_ids=[0])
    return r.results[0]["out"]
```
